# Optimizing a Trainium2 kernel written in Bass

```python
import numpy as np
import jax
import jax.numpy as jnp

def _softmax(x, axis=-1):
    return jax.nn.softmax(x, axis=axis)

def _gelu(x):
    return jax.nn.gelu(x, approximate=True)

def _silu(x):
    return jax.nn.silu(x)

def _sigmoid(x):
    return jax.nn.sigmoid(x)

def _layernorm(x, axis=-1, eps=1e-05):
    m = jnp.mean(x, axis=axis, keepdims=True)
    v = jnp.var(x, axis=axis, keepdims=True)
    return (x - m) / jnp.sqrt(v + eps)

def _scatter_add(tgt, idx, src, axis=0):
    return tgt.at[idx].add(src)

def _segment_sum(src, seg, n):
    return jax.ops.segment_sum(src, seg, n)
kernel_name = 'mk_flamingo_gated_d1_seqx_r4_ea3924'

def setup_inputs(seed: int=0):
    np.random.seed(seed)
    _w = jnp.asarray

    def _rec_inputs():
        import jax
        import jax.numpy as jnp
        _rk = jax.random.key(seed)
        x = -0.0002928 + 1 * jax.random.normal(jax.random.fold_in(_rk, 1), (4, 512, 256), jnp.float32)
        _lenS = 512 - jax.random.randint(jax.random.fold_in(_rk, 7), (4,), 0, max(1, 512 // 4) + 1, jnp.int32)
        _lenS2 = 512 - jax.random.randint(jax.random.fold_in(_rk, 8), (4,), 0, max(1, 512 // 4) + 1, jnp.int32)
        _ctx_1024P = jax.random.normal(jax.random.fold_in(_rk, 11), (4, 16, 256), jnp.float32)
        _ctx_1024c = jax.random.dirichlet(jax.random.fold_in(_rk, 511), 0.3 * jnp.ones((16,), jnp.float32), (4, 512))
        _ctx_1024t = jnp.einsum('bsk,bkd->bsd', _ctx_1024c, _ctx_1024P)
        _ctx_1024t = _ctx_1024t * jax.lax.rsqrt(jnp.mean(jnp.square(_ctx_1024t)) + 1e-12) * 0.953939
        ctx_1024 = -1.39393e-06 + 0.999914 * (_ctx_1024t + 0.3 * jax.random.normal(jax.random.fold_in(_rk, 611), (4, 512, 256), jnp.float32))
        _g = jax.random.normal(jax.random.fold_in(_rk, 9001), (2, 1), jnp.float32)
        _g = jnp.sign(_g) * jnp.maximum(jnp.abs(_g), 1.0) + (_g == 0) * 1.0
        g_xattn = _g[0]
        g_ffn = _g[1]
        return (x, ctx_1024, g_xattn, g_ffn)
    x, ctx_1024, g_xattn, g_ffn = _rec_inputs()

    def _L0_xattn_setup():
        import jax, jax.numpy as jnp
        import numpy as np
        B, TQ, TK = (2, 512, 512)
        X_TO_DIM = 256
        X_FROM_DIM = 256
        HIDDEN = 256
        H = 16
        DH = HIDDEN // H
        key = jax.random.key(seed)
        ks = jax.random.split(key, 10)
        s = 0.02
        return {'x_to': jax.random.normal(ks[0], (B, TQ, X_TO_DIM), dtype=jnp.float32), 'x_from': jax.random.normal(ks[1], (B, TK, X_FROM_DIM), dtype=jnp.float32), 'Wq': jax.random.normal(ks[2], (H, X_TO_DIM, DH), dtype=jnp.float32) * s, 'bq': jax.random.normal(ks[3], (H, DH), dtype=jnp.float32) * s, 'Wk': jax.random.normal(ks[4], (H, X_FROM_DIM, DH), dtype=jnp.float32) * s, 'bk': jax.random.normal(ks[5], (H, DH), dtype=jnp.float32) * s, 'Wv': jax.random.normal(ks[6], (H, X_FROM_DIM, DH), dtype=jnp.float32) * s, 'bv': jax.random.normal(ks[7], (H, DH), dtype=jnp.float32) * s, 'Wo': jax.random.normal(ks[8], (HIDDEN, HIDDEN), dtype=jnp.float32) * s, 'bo': jax.random.normal(ks[9], (HIDDEN,), dtype=jnp.float32) * s}
    _L0_xattn_all = _L0_xattn_setup()
    _L0_xattn_in = {k: v for k, v in _L0_xattn_all.items() if k in ('Wq', 'bq', 'Wk', 'bk', 'Wv', 'bv', 'Wo', 'bo')}
    del _L0_xattn_all

    def _L0_ffn_setup():
        import jax, jax.numpy as jnp
        import numpy as np
        NUM_EXPERTS = 8
        TOP_K = 2
        key = jax.random.key(seed)
        ks = jax.random.split(key, 5)
        B, L, E, H, N = (2, 512, 256, 512, NUM_EXPERTS)
        return {'x': jax.random.normal(ks[0], (B, L, E), dtype=jnp.float32), 'gate_kernel': jax.random.normal(ks[1], (E, N), dtype=jnp.float32) / np.sqrt(E), 'w0_kernel': jax.random.normal(ks[2], (N, E, H), dtype=jnp.float32) / np.sqrt(E), 'w1_kernel': jax.random.normal(ks[3], (N, E, H), dtype=jnp.float32) / np.sqrt(E), 'wo_kernel': jax.random.normal(ks[4], (N, H, E), dtype=jnp.float32) / np.sqrt(H)}
    _L0_ffn_all = _L0_ffn_setup()
    _L0_ffn_in = {k: v for k, v in _L0_ffn_all.items() if k in ('gate_kernel', 'w0_kernel', 'w1_kernel', 'wo_kernel')}
    del _L0_ffn_all
    return {'x': x, 'ctx_1024': ctx_1024, 'g_xattn': g_xattn, 'g_ffn': g_ffn, 'L0_xattn_Wq': _L0_xattn_in['Wq'], 'L0_xattn_bq': _L0_xattn_in['bq'], 'L0_xattn_Wk': _L0_xattn_in['Wk'], 'L0_xattn_bk': _L0_xattn_in['bk'], 'L0_xattn_Wv': _L0_xattn_in['Wv'], 'L0_xattn_bv': _L0_xattn_in['bv'], 'L0_xattn_Wo': _L0_xattn_in['Wo'], 'L0_xattn_bo': _L0_xattn_in['bo'], 'L0_ffn_gate_kernel': _L0_ffn_in['gate_kernel'], 'L0_ffn_w0_kernel': _L0_ffn_in['w0_kernel'], 'L0_ffn_w1_kernel': _L0_ffn_in['w1_kernel'], 'L0_ffn_wo_kernel': _L0_ffn_in['wo_kernel']}

def reference(x, ctx_1024, g_xattn, g_ffn, L0_xattn_Wq, L0_xattn_bq, L0_xattn_Wk, L0_xattn_bk, L0_xattn_Wv, L0_xattn_bv, L0_xattn_Wo, L0_xattn_bo, L0_ffn_gate_kernel, L0_ffn_w0_kernel, L0_ffn_w1_kernel, L0_ffn_wo_kernel):
    import jax
    import jax.numpy as jnp

    def _L0_xattn_ref(x_to, x_from, Wq, bq, Wk, bk, Wv, bv, Wo, bo):
        import jax, jax.numpy as jnp
        import numpy as np
        B, TQ, TK = (2, 512, 512)
        X_TO_DIM = 256
        X_FROM_DIM = 256
        HIDDEN = 256
        H = 16
        DH = HIDDEN // H
        q = jnp.einsum('btf,hfd->bhtd', x_to, Wq) + bq[None, :, None, :]
        k = jnp.einsum('bsf,hfd->bhsd', x_from, Wk) + bk[None, :, None, :]
        v = jnp.einsum('bsf,hfd->bhsd', x_from, Wv) + bv[None, :, None, :]
        scores = jnp.einsum('bhtd,bhsd->bhts', q, k) / jnp.sqrt(jnp.float32(DH))
        attn = jax.nn.softmax(scores, axis=-1)
        out = jnp.einsum('bhts,bhsd->bhtd', attn, v)
        concat = jnp.transpose(out, (0, 2, 1, 3)).reshape(out.shape[0], out.shape[2], H * DH)
        return concat @ Wo.T + bo

    def _L0_ffn_ref(x, gate_kernel, w0_kernel, w1_kernel, wo_kernel):
        import jax, jax.numpy as jnp
        import numpy as np
        NUM_EXPERTS = 8
        TOP_K = 2
        B, L, E = x.shape
        gate_logits = jnp.einsum('ble,en->bln', x, gate_kernel)
        top_k_weights, top_k_indices = jax.lax.top_k(gate_logits, TOP_K)
        softmax_probs = jax.nn.softmax(top_k_weights.astype(jnp.float32), axis=-1)
        weights = jnp.zeros_like(gate_logits)
        b_idx = jnp.arange(B)[:, None, None]
        l_idx = jnp.arange(L)[:, None]
        weights = weights.at[b_idx, l_idx, top_k_indices].set(softmax_probs)
        layer_w0 = jnp.einsum('ble,neh->blnh', x, w0_kernel)
        layer_w1 = jnp.einsum('ble,neh->blnh', x, w1_kernel)
        layer_mult = jax.nn.silu(layer_w0) * layer_w1
        intermediate = jnp.einsum('blnh,nhe->blne', layer_mult, wo_kernel)
        output = jnp.einsum('blne,bln->ble', intermediate, weights)
        return output
    x = x + jnp.tanh(g_xattn[0]) * _L0_xattn_ref(_layernorm(x, axis=-1), ctx_1024, L0_xattn_Wq, L0_xattn_bq, L0_xattn_Wk, L0_xattn_bk, L0_xattn_Wv, L0_xattn_bv, L0_xattn_Wo, L0_xattn_bo)
    x = x + jnp.tanh(g_ffn[0]) * _L0_ffn_ref(_layernorm(x, axis=-1), L0_ffn_gate_kernel, L0_ffn_w0_kernel, L0_ffn_w1_kernel, L0_ffn_wo_kernel)
    return x

_drawn_inputs = setup_inputs


def setup_inputs(seed=0):
    import zlib

    import numpy as np

    out = dict(_drawn_inputs(seed))
    spreads = {}
    factors = {'L0_xattn_Wq': 8.0,
     'L0_xattn_bq': 8.0,
     'L0_xattn_Wk': 4.507,
     'L0_xattn_bk': 8.0,
     'L0_xattn_bv': 2.699}
    for name, (base, spread) in spreads.items():
        noise = np.random.default_rng([zlib.crc32(name.encode()), seed]).standard_normal(out[name].shape)
        drawn = base * np.exp(spread * noise) if base else spread * noise
        out[name] = jnp.asarray(drawn.astype(out[name].dtype))
    for name, factor in factors.items():
        out[name] = (out[name] * factor).astype(out[name].dtype)
    return out
```

```python
import concourse.bass as bass
from concourse import mybir
from contextlib import ExitStack

F32 = mybir.dt.float32
F16 = mybir.dt.float16
I32 = mybir.dt.int32
U32 = mybir.dt.uint32
ALU = mybir.AluOpType
ACT = mybir.ActivationFunctionType
AX_X = mybir.AxisListType.X

P = 128
EPS = 1e-5
WSCALE = 16.0
MSCALE = 256.0


def program(nc, x, ctxT, g_xattn, g_ffn, wq, bq, wk, bk, wv, bv, woT, bo, gate, w0, w1, wo, out):
    TOKENS, D = x.shape
    B, _, S = ctxT.shape
    KD = D // P
    TT = S // P
    TILES = TOKENS // P
    H = 16
    DH = D // H
    G = 4
    NG = H // G
    VW = DH + 1
    KS_ROWS = 3 * DH
    SLOTS = NG * TT
    _, NE = gate.shape
    HID = w0.shape[2]
    KH = HID // P
    REGION = TOKENS
    NT = (2 * TOKENS + NE * (P - 1)) // P
    SPARE = (NE - 1) * REGION + NT * P
    SCORE_SCALE = 1.0 / (float(DH) ** 0.5 * WSCALE * WSCALE)

    with ExitStack() as ctx:
        def sb(name, shape, dt):
            return ctx.enter_context(nc.sbuf_tensor(name, shape, dt))

        def psum(name, shape, dt=F32):
            return ctx.enter_context(nc.psum_tensor(name, shape, dt))

        def sem(name):
            return ctx.enter_context(nc.semaphore(name))

        ident = sb("ident", [P, P], F32)
        WE = sb("WE", [P, NE, 6, KD * HID], F16)
        last_expert = WE[:, NE - 1, :, :].rearrange("p a n -> p (a n)")
        X = sb("X", [P, TILES, D], F32)
        stage = sb("stage", [P, 4, KD, D], F32)
        wh = sb("wh", [P, 4, KD, D], F16)
        wl = sb("wl", [P, 4, KD, D], F16)
        bq_s = sb("bq_s", [P, 2, 2], F32)
        bv_b = sb("bv_b", [P, D], F32)
        bo_b = sb("bo_b", [P, D], F32)
        gains = sb("gains", [P, 2], F32)
        tg = sb("tg", [P, 2], F32)
        tg16 = sb("tg16", [P, 2], F32)
        st6 = sb("st6", [P, TILES, 6], F32)
        mv = sb("mv", [P, TILES, 2], F32)
        sd = sb("sd", [P, TILES], F32)
        nw = sb("nw", [P, 2, TILES], F32)
        rstd = sb("rstd", [P, TILES], F32)
        xn = sb("xn", [P, TT, D], F32)
        xth = sb("xth", [P, KD, S], F16)
        xtl = sb("xtl", [P, KD, S], F16)
        c32 = sb("c32", [P, KD, S], F32)
        cth = last_expert[:, 4096:5120].rearrange("p (k s) -> p k s", k=KD)
        ctl = last_expert[:, 5120:6144].rearrange("p (k s) -> p k s", k=KD)
        nat = sb("nat", [P, 2, 2, 2, S], F16)
        QS = last_expert[:, 0:4096].rearrange("p (h s) -> p h s", h=H // 2)
        KS = sb("KS", [P, H // 2, S], F16)
        V = sb("V", [P, 2, TT, H, VW], F32)
        mx = sb("mx", [P, 2, TT, G], F32)
        mrow = sb("mrow", [G, NG, S], F16)
        E = sb("E", [P, 4, 2, S], F32)
        OT = sb("OT", [P, 2, S], F32)
        rec = sb("rec", [P, TT, G], F32)
        att = sb("att", [P, TT, D], F32)
        ath = sb("ath", [P, KD, S], F16)
        atl = sb("atl", [P, KD, S], F16)

        g32 = sb("g32", [P, KD, NE], F32)
        gh = sb("gh", [P, KD, NE], F16)
        gl = sb("gl", [P, KD, NE], F16)
        earlier = sb("earlier", [P, P], F16)
        ones = sb("ones", [P, P], F16)
        iota_e = sb("iota_e", [P, NE], F32)
        iota_t = sb("iota_t", [1, NT], F32)
        token = sb("token", [P, TILES], I32)
        zeros = sb("zeros", [P, SPARE // P], I32)
        lg = sb("lg", [P, TT, NE], F32)
        m8 = sb("m8", [P, TT, 8], F32)
        i8 = sb("i8", [P, TT, 8], U32)
        idf = sb("idf", [P, TT, 2], F32)
        pick = sb("pick", [P, 2, TILES, NE], F32)
        both = sb("both", [P, TT, NE], F16)
        gap = sb("gap", [P, TT], F32)
        egap = sb("egap", [P, TT], F32)
        den = sb("den", [P, TT], F32)
        share = sb("share", [P, TILES, 2], F32)
        next_slot = sb("next_slot", [P, NE], F32)
        slot_of = sb("slot_of", [P, TT, NE], F32)
        chosen = sb("chosen", [P, TT, NE], F32)
        slot = sb("slot", [P, 2, TILES], I32)
        cnt = sb("cnt", [P, NE], F32)
        cnt_i = sb("cnt_i", [P, 2, NE], I32)
        ntile = sb("ntile", [P, NE], F32)
        cum = sb("cum", [P, 2, NE], F32)
        attf = att[:, :, :].rearrange("p t d -> p (t d)")
        before = attf[0:1, 0:2 * NT * (NE - 1)].rearrange("p (a t e) -> p a t e", a=2, t=NT)
        tile_f = sb("tile_f", [1, 3, NT], F32)
        tile_e = sb("tile_e", [1, NT], I32)
        tile_s = sb("tile_s", [1, NT], I32)
        shift = sb("shift", [P, NE], F32)
        shifted = attf[:, 640:640 + 2 * TILES * NE].rearrange("p (k t e) -> p k t e", k=2, t=TILES)
        back_f = sb("back_f", [P, 2, TILES], F32)
        back = sb("back", [P, 2, TILES], I32)
        slots_f = sb("slots_f", [P, 2, TILES], F32)
        ids = sb("ids", [P, 2, 1], U32)
        Ef = E[:, :, :, :].rearrange("p a b n -> p (a b n)")
        xg = Ef[:, 0:512].rearrange("p (b d) -> p b d", b=2)
        silu = Ef[:, 512:1536].rearrange("p (b n) -> p b n", b=2)
        mid = Ef[:, 1536:2560].rearrange("p (b n) -> p b n", b=2)
        ysb = Ef[:, 2560:3072].rearrange("p (b n) -> p b n", b=2)
        natf = nat[:, :, :, :, :].rearrange("p a b c n -> p (a b c n)")
        xs = natf[:, 0:1024].rearrange("p (b h n) -> p b h n", b=2, h=2)
        ms = natf[:, 1024:3072].rearrange("p (b h n) -> p b h n", b=2, h=2)
        gy = WE[:, :, :, :].rearrange("p a b n -> p (a b n)")[:, 0:4 * TILES * D].bitcast(F32).rearrange(
            "p (t k d) -> p t k d", t=TILES, k=2)
        rows_d = nc.dram_tensor("rows_by_token", (TOKENS, D), F32, kind="Internal").ap()
        ids_d = nc.dram_tensor("token_by_slot", (SPARE, 1), I32, kind="Internal").ap()
        y_d = nc.dram_tensor("output_by_tile", (NT * P, D), F32, kind="Internal").ap()

        SC = psum("SC", [P, 2, 2, S])
        PV = psum("PV", [P, S])
        NB = 3
        WB = psum("WB", [P, NB, 512])
        HB = SC
        TX, TM, YB = WB[:, 0, :], WB[:, 1, :], (WB[:, 2, :], PV)

        s_x0 = sem("x_first_batch_loaded")
        s_x = sem("x_other_batches_loaded")
        s_w = sem("attention_weights_loaded")
        s_small = sem("biases_and_gains_loaded")
        s_ctx = sem("context_loaded")
        s_ident = sem("identity_made")
        s_vone = sem("value_ones_set")
        s_wh = sem("weight_high_parts_made")
        s_wl = sem("weight_low_parts_made")
        s_ctsplit = sem("context_split")
        s_bias = sem("biases_scaled")
        s_tanh = sem("gains_tanh_made")
        s_stats = sem("variances_ready")
        s_sqrt = sem("deviations_ready")
        s_xn = sem("rows_normalised")
        s_xbo = sem("output_bias_added")
        s_fill = sem("work_bank_filled")
        s_free = sem("work_bank_emptied")
        s_dve = sem("vector_step_done")
        s_pool = sem("pool_step_done")
        s_stack = [sem(f"group{g}_stacked") for g in range(NG)]
        s_mrow = [sem(f"group{g}_maxima_placed") for g in range(NG)]
        s_score = sem("scores_done")
        s_exp = sem("exponentials_done")
        s_pv = sem("values_weighted")
        s_ot = sem("attention_output_copied")
        s_pz = sem("output_bank_zeroed")
        s_out = sem("result_stored")
        s_gate = sem("router_weights_loaded")
        s_gsplit = sem("router_weights_split")
        s_const = sem("router_constants_made")
        s_zero = sem("token_table_cleared")
        s_rows = sem("rows_stored")
        s_gap = sem("choice_gaps_ready")
        s_egap = sem("choice_gaps_exponentiated")
        s_xhigh = sem("tile_high_part_made")
        s_mhigh = sem("middle_high_part_made")
        s_stats2 = sem("expert_input_variances_ready")
        s_sqrt2 = sem("expert_input_deviations_ready")
        s_xn2 = sem("expert_input_normalised")
        s_share = sem("choices_weighed")
        s_slot = sem("slots_numbered")
        s_idput = sem("tokens_placed")
        s_tiles = sem("tiles_listed")
        s_backrow = sem("output_rows_worked_out")
        s_we = [sem(f"expert_weights_loaded{i}") for i in range(2)]
        s_wsplit = sem("expert_weights_split")
        s_last_high = sem("last_expert_high_parts_made")
        s_last_low = sem("last_expert_low_parts_made")
        s_ids = [sem(f"tile_tokens_loaded{i}") for i in range(2)]
        s_xg = [sem(f"tile_rows_gathered{i}") for i in range(2)]
        s_tx = sem("tile_turned")
        s_xs = sem("tile_split")
        s_h = sem("hidden_sums_done")
        s_silu = sem("silu_done")
        s_mid = sem("middle_done")
        s_tm = sem("middle_turned")
        s_ms = sem("middle_split")
        s_y = sem("expert_output_done")
        s_ysb = sem("expert_output_copied")
        s_yd = [sem(f"expert_output_stored{i}") for i in range(2)]
        s_back = [sem(f"outputs_gathered{i}") for i in range(TILES // TT)]
        s_sum = sem("result_summed")

        slot_units = {s: [] for s in range(-1, B * SLOTS + 12)}

        def place(s, *unit):
            slot_units[s].append(unit)

        for b in range(B):
            base = SLOTS * (b - 1)
            at = (lambda o: -1) if b == 0 else (lambda o: base + o)
            for k in range(KD):
                place(at(0 + k), "xt", b, k)
            for c in range(2):
                place(at(2 + c), "k", b, c)
                place(at(2 + c), "q", b, c)
            for h in range(2):
                place(at(4 + h), "v", b, h)
        early = {(0, 0): (-1, -1), (0, 1): (0, 2), (0, 2): (2, 5), (0, 3): (5, 8)}
        for b in range(B):
            for g in range(NG):
                home = SLOTS * b + 4 * g
                first, last = early.get((b, g), (home - 10, home - 7))
                for n in range(TT * G):
                    place(first + (last - first + 1) * n // (TT * G), "max", b, g, n // G, n % G)
                place(last, "mt", b, g)
                place(home + 5, "ot", b, g)
        for b in range(B):
            end = SLOTS * (b + 1)
            for c in range(2):
                place(end + 2, "at", b, c)
            for h in range(2):
                place(end + 3, "wo", b, h)
            for k in range(KD):
                place(end + 5, "xt2", b, k)
            place(end + 6, "gate", b)
            place(end + 8, "rank", b)
        order = [u for s in sorted(slot_units) for u in slot_units[s]]
        number = {u: n for n, u in enumerate(order)}

        def emptied(eng, *unit):
            eng.wait_ge(s_free, number[unit] + 1)

        def since(i, first):
            return not isinstance(i, int) or i >= first

        def part_stage(n):
            return stage[:, 2 * (n % 2):2 * (n % 2) + 2, :, :].rearrange("p a k n -> p (a k n)")

        block = ctx.enter_context(nc.Block())

        @block.sync
        def _(sp):
            xr = x.rearrange("(t p) d -> p t d", p=P)
            sp.dma_start(X[:, 0:TT, :], xr[:, 0:TT, :]).then_inc(s_x0, 16)
            for n, w in enumerate((wk, wq, wv, woT)):
                n = (1, 0, 2, 3)[n]
                sp.dma_start(stage[:, n, :, :], w.rearrange("(k p) n -> p k n", p=P)).then_inc(s_w, 16)
            sp.dma_start(X[:, TT:TILES, :], xr[:, TT:TILES, :]).then_inc(s_x, 16)
            for n, v in enumerate((bq, bk)):
                sp.dma_start(bq_s[:, n, :], v).then_inc(s_small, 16)
            for t, v in ((bv_b, bv), (bo_b, bo)):
                sp.dma_start(t[:, :], v.rearrange("(a n) -> a n", a=1).broadcast_to([P, D])).then_inc(s_small, 16)
            sp.dma_start(g32[:, :, :], gate.rearrange("(k p) n -> p k n", p=P)).then_inc(s_gate, 16)
            for n, v in enumerate((g_xattn, g_ffn)):
                sp.dma_start(gains[:, n:n + 1], v.rearrange("(a n) -> a n", a=1).broadcast_to([P, 1])).then_inc(s_small, 16)

            def stack(b, g):
                if b:
                    sp.wait_ge(s_score, 2 * (SLOTS * (b - 1) + TT * (g + 1)))
                if g == 0:
                    emptied(sp, "q", b, 1)
                for r in range(2):
                    i = 2 * g + r
                    for t, (dst, parts) in enumerate(((QS, (0, 0, 1)), (KS, (0, 1, 0)))):
                        for o, hl in enumerate(parts):
                            row = 64 * r + DH * o
                            sp.dma_start(dst[row:row + DH, 2 * g:2 * g + 2, :],
                                         nat[DH * i:DH * i + DH, t, hl, :, :]).then_inc(s_stack[g], 16)

            def maxima(b, g):
                emptied(sp, "mt", b, g)
                for r in range(2):
                    row = 64 * r + KS_ROWS
                    sp.dma_start(QS[row:row + 1, 2 * g:2 * g + 2, :],
                                 mrow[2 * r:2 * r + 2, g, :]).then_inc(s_mrow[g], 16)

            def store_rows(b, g):
                sp.wait_ge(s_xn2, b + 1)
                sp.dma_start(rows_d.rearrange("(t p) d -> p t d", p=P)[:, TT * b:TT * (b + 1), :],
                             xn[:, :, :]).then_inc(s_rows, 16)

            sp.wait_ge(s_const, 1)
            sp.dma_start(ids_d.rearrange("(p n) a -> p (n a)", p=P), zeros[:, :]).then_inc(s_zero, 16)
            jobs = []
            for b in range(B):
                jobs.append((SLOTS * (b + 1) + 5, 2, store_rows, b, 0))
                for g in range(NG):
                    home = SLOTS * b + 4 * g
                    jobs.append((home - 12 if b else -2, 0, stack, b, g))
                    jobs.append((early.get((b, g), (0, home - 7))[1], 1, maxima, b, g))
            for _, _, job, b, g in sorted(jobs, key=lambda j: (j[0], j[1], j[3], j[4])):
                job(b, g)

            def load_tokens(i, par):
                if since(i, 2):
                    sp.wait_ge(s_xg[par], i * 8 - 8 * par)
                at = sp.value_load(tile_s[0:1, bass.ds(i, 1)], min_val=0, max_val=SPARE - P)
                sp.dma_start(ids[:, par, :], ids_d[bass.ds(at, P), :].bitcast(U32)).then_inc(s_ids[par], 16)

            def store_output(i, par):
                sp.wait_ge(s_ysb, i + 1)
                sp.dma_start(y_d[bass.ds(i * P, P), :], ysb[:, par, :]).then_inc(s_yd[par], 16)

            sp.wait_ge(s_idput, 16 * 2 * TILES)
            sp.wait_ge(s_tiles, 1)
            LAG = 5
            for i in range(LAG):
                load_tokens(i, i % 2)
            with sp.Fori(LAG, NT - 1, 2) as i:
                for o in range(2):
                    load_tokens(i + o, (LAG + o) % 2)
                    store_output(i + o - LAG, o)
            for i in range(NT - LAG, NT):
                store_output(i, i % 2)
            for b in range(B):
                sp.wait_ge(s_sum, b + 1)
                sp.dma_start(out.rearrange("(t p) d -> p t d", p=P)[:, TT * b:TT * (b + 1), :],
                             X[:, TT * b:TT * (b + 1), :]).then_inc(s_out, 16)
            sp.wait_ge(s_out, 16 * B)

        @block.gpsimd
        def _(pool):
            steps = [0]

            def step(ins):
                steps[0] += 1
                ins.then_inc(s_pool, 1)
                pool.wait_ge(s_pool, steps[0])

            pool.dma_start(c32[:, :, :], ctxT[0].rearrange("(k p) s -> p k s", p=P)).then_inc(s_ctx, 16)
            step(nc.gpsimd.memset(ident[:, :], 0.0))
            nc.gpsimd.affine_select(out=ident[:, :], in_=ident[:, :], compare_op=ALU.not_equal, fill=1.0,
                                    base=0, pattern=[[-1, P]], channel_multiplier=1).then_inc(s_ident, 1)
            pool.wait_ge(s_ident, 1)
            nc.gpsimd.memset(KS[32:64, :, :], -MSCALE).then_inc(s_vone, 1)
            pool.wait_ge(s_vone, 1)
            nc.gpsimd.memset(KS[96:128, :, :], -MSCALE).then_inc(s_vone, 1)
            pool.wait_ge(s_vone, 2)
            nc.gpsimd.memset(V[:, :, :, :, :], 1.0).then_inc(s_vone, 1)
            pool.wait_ge(s_vone, 3)
            step(nc.gpsimd.memset(zeros[:, :], 0))
            step(nc.gpsimd.memset(ones[:, :], 1.0))
            step(nc.gpsimd.memset(earlier[:, :], 1.0))
            step(nc.gpsimd.affine_select(out=earlier[:, :], in_=earlier[:, :], compare_op=ALU.is_gt, fill=0.0,
                                         base=0, pattern=[[1, P]], channel_multiplier=-1))
            step(nc.gpsimd.iota(iota_e[:, :], pattern=[[1, NE]], base=0, channel_multiplier=0,
                                allow_small_or_imprecise_dtypes=True))
            step(nc.gpsimd.iota(iota_t[:, :], pattern=[[1, NT]], base=0, channel_multiplier=0,
                                allow_small_or_imprecise_dtypes=True))
            step(nc.gpsimd.iota(next_slot[:, :], pattern=[[REGION, NE]], base=0, channel_multiplier=0,
                                allow_small_or_imprecise_dtypes=True))
            nc.gpsimd.iota(token[:, :], pattern=[[P, TILES]], base=0, channel_multiplier=1).then_inc(s_const, 1)

            def load_part(n):
                e, m = divmod(n, 3)
                src = (w0, w1, wo)[m][e]
                pool.dma_start(part_stage(n).rearrange("p (k n) -> p k n", n=src.shape[1]),
                               src.rearrange("(k p) n -> p k n", p=P)).then_inc(s_we[n % 2], 16)

            def split_part(n):
                e, m = divmod(n, 3)
                pool.wait_ge(s_we[n % 2], 16 * (n // 2 + 1))
                w = part_stage(n)
                step(nc.gpsimd.tensor_scalar(w, w, WSCALE, None, ALU.mult))
                step(nc.gpsimd.tensor_copy(WE[:, e, 2 * m, :], w))
                nc.gpsimd.tensor_tensor(WE[:, e, 2 * m + 1, :], w, WE[:, e, 2 * m, :], ALU.subtract).then_inc(s_wsplit, 1)
                pool.wait_ge(s_wsplit, n + 1)
                load_part(n + 2)

            def place_tokens(b):
                pool.wait_ge(s_slot, b + 1)
                if b == 0:
                    pool.wait_ge(s_zero, 16)
                for t in range(TT * b, TT * (b + 1)):
                    for k in range(2):
                        pool.indirect_dma_start(ids_d[:, :], bass.IndirectOffsetOnAxis(slot[:, k, t:t + 1].bitcast(U32), 0),
                                                token[:, t:t + 1], None).then_inc(s_idput, 16)

            parts = [6, 5, 5, 5]
            todo = 0
            for b in range(B):
                pool.wait_ge(s_ctx, 16 * (b + 1))
                if b:
                    emptied(pool, "v", b - 1, 1)
                step(nc.gpsimd.tensor_copy(cth[:, :, :], c32[:, :, :]))
                nc.gpsimd.tensor_tensor(ctl[:, :, :], c32[:, :, :], cth[:, :, :], ALU.subtract).then_inc(s_ctsplit, 1)
                if b + 1 < B:
                    pool.wait_ge(s_ctsplit, b + 1)
                    pool.dma_start(c32[:, :, :], ctxT[b + 1].rearrange("(k p) s -> p k s", p=P)).then_inc(s_ctx, 16)
                pool.wait_ge(s_xn, b + 1)
                if b == 0:
                    pool.wait_ge(s_bias, 1)
                rows = X[:, TT * b:TT * (b + 1), :]
                nc.gpsimd.tensor_tensor(rows, rows, bo_b[:, :].rearrange("p (a d) -> p a d", a=1).broadcast_to([P, TT, D]),
                                        ALU.add).then_inc(s_xbo, 1)
                if b == 0:
                    pool.wait_ge(s_wl, 1)
                    load_part(0)
                    load_part(1)
                else:
                    if b > 1:
                        place_tokens(b - 2)
                for _ in range(parts[b]):
                    split_part(todo)
                    todo += 1
            pool.wait_ge(s_last_low, 1)
            load_part(3 * NE - 1)
            place_tokens(2)
            place_tokens(3)

            def gather(i, par):
                pool.wait_ge(s_ids[par], i * 8 - 8 * par + 16)
                if since(i, 2):
                    pool.wait_ge(s_tx, i - 1)
                pool.wait_ge(s_rows, 16 * B)
                pool.indirect_dma_start(xg[:, par, :], None, rows_d[:, :],
                                        bass.IndirectOffsetOnAxis(ids[:, par, :], 0)).then_inc(s_xg[par], 16)

            pool.wait_ge(s_pv, B * SLOTS)
            for i in range(NT):
                gather(i, i % 2)
            pool.wait_ge(s_backrow, 1)
            for par in range(2):
                pool.wait_ge(s_yd[par], 16 * ((NT + 1 - par) // 2))
            for t in range(TILES):
                for k in range(2):
                    pool.indirect_dma_start(gy[:, t, k, :], None, y_d[:, :],
                                            bass.IndirectOffsetOnAxis(back[:, k, t:t + 1].bitcast(U32), 0)
                                            ).then_inc(s_back[t // TT], 16)

        @block.scalar
        def _(act):
            def copy_output(act, q):
                act.wait_ge(s_pv, TT * (q + 1))
                if q >= 2:
                    emptied(act, "ot", (q - 2) // NG, (q - 2) % NG)
                nc.scalar.activation(OT[:, q % 2, :], PV[:, :], ACT.Copy).then_inc(s_ot, 1)

            def second_norm(b):
                act.wait_ge(s_stats2, b + 1)
                nc.scalar.activation(sd[:, TT * b:TT * (b + 1)], nw[:, 0, TT * b:TT * (b + 1)], ACT.Sqrt).then_inc(s_sqrt2, 1)

            def choice_exp(b):
                act.wait_ge(s_gap, b + 1)
                nc.scalar.activation(egap[:, :], gap[:, :], ACT.Exp).then_inc(s_egap, 1)

            act.wait_ge(s_small, 16 * 6)
            nc.scalar.activation(tg[:, :], gains[:, :], ACT.Tanh).then_inc(s_tanh, 1)
            act.wait_ge(s_w, 16 * 4)
            nc.scalar.activation(wh[:, :, :, :], stage[:, :, :, :], ACT.Copy, scale=WSCALE).then_inc(s_wh, 1)
            for n, (lo, hi) in enumerate(((0, TT), (TT, TILES))):
                act.wait_ge(s_stats, n + 1)
                nc.scalar.activation(sd[:, lo:hi], nw[:, 0, lo:hi], ACT.Sqrt).then_inc(s_sqrt, 1)
            for n in range(2 * B * SLOTS):
                act.wait_ge(s_score, n + 1)
                if n >= 4:
                    act.wait_ge(s_pv, (n - 4) // 2 + 1)
                nc.scalar.activation(E[:, n % 4, :, :], SC[:, n % 2, :, :], ACT.Exp,
                                     scale=SCORE_SCALE).then_inc(s_exp, 1)
                s, half = divmod(n, 2)
                if half == 1 and s % TT == 0 and s:
                    copy_output(act, s // TT - 1)
                if half == 1 and s >= SLOTS and s % SLOTS == 4:
                    second_norm(s // SLOTS - 1)
                if half == 1 and s >= SLOTS and s % SLOTS == 7:
                    choice_exp(s // SLOTS - 1)
            copy_output(act, B * NG - 1)
            for n in range(3):
                act.wait_ge(s_we[(3 * NE - 3 + n) % 2], 16 * ((3 * NE - 3 + n) // 2 + 1))
                if n == 0:
                    emptied(act, "v", B - 1, 1)
                nc.scalar.activation(WE[:, NE - 1, 2 * n, :], part_stage(3 * NE - 3 + n), ACT.Copy,
                                     scale=WSCALE).then_inc(s_last_high, 1)
            second_norm(B - 1)
            choice_exp(B - 1)

            def hidden(i, par):
                act.wait_ge(s_h, i + 1)
                if since(i, 2):
                    act.wait_ge(s_mid, i - 1)
                nc.scalar.activation(silu[:, par, :], HB[:, par, 0, :], ACT.Silu, scale=1.0 / WSCALE).then_inc(s_silu, 1)

            def output(i, par):
                act.wait_ge(s_y, i + 1)
                if since(i, 2):
                    act.wait_ge(s_yd[par], i * 8 - 8 * par)
                nc.scalar.activation(ysb[:, par, :], YB[par][:, 0:D], ACT.Copy).then_inc(s_ysb, 1)

            def expert_step(i, par):
                if not (isinstance(i, int) and i >= NT):
                    hidden(i, par)
                if since(i, 2):
                    output(i - 2, par)

            for i in range(4):
                expert_step(i, i % 2)
            with act.Fori(4, NT - 1, 2) as i:
                for o in range(2):
                    expert_step(i + o, o)
            for i in range(NT - 1, NT + 2):
                expert_step(i, i % 2)

        @block.vector
        def _(dve):
            steps = [0]

            def step(ins):
                steps[0] += 1
                ins.then_inc(s_dve, 1)
                dve.wait_ge(s_dve, steps[0])

            def stats(lo, hi, ready):
                for t in range(lo, hi):
                    last = nc.vector.bn_stats(st6[:, t, :], X[:, t, :])
                step(last)
                for t in range(lo, hi):
                    last = nc.vector.bn_aggr(mv[:, t, :], st6[:, t, :])
                step(last)
                nc.vector.tensor_scalar(nw[:, 0, lo:hi], mv[:, lo:hi, 1], EPS, None, ALU.add).then_inc(ready, 1)

            def inverse_deviation(lo, hi, s_root, n):
                dve.wait_ge(s_root, n)
                v, a, r = nw[:, 0, lo:hi], nw[:, 1, lo:hi], rstd[:, lo:hi]
                step(nc.vector.reciprocal(r, sd[:, lo:hi]))
                step(nc.vector.tensor_tensor(a, r, r, ALU.mult))
                step(nc.vector.tensor_tensor(a, a, v, ALU.mult))
                step(nc.vector.tensor_scalar(a, a, -0.5, 1.5, ALU.mult, ALU.add))
                step(nc.vector.tensor_tensor(r, r, a, ALU.mult))

            def normalise(b, ready):
                if ready is s_xn2:
                    dve.wait_ge(s_fill, number["xt", min(b + 2, B - 1), 1] + 1)
                    stored = b
                else:
                    if b:
                        dve.wait_ge(s_fill, number["xt", b - 1, 1] + 1)
                    stored = b - 2
                if stored > 0:
                    dve.wait_ge(s_fill, number["xt2", stored - 1, 1] + 1)
                    dve.wait_ge(s_rows, 16 * stored)
                for t in range(TT):
                    n = TT * b + t
                    last = nc.vector.tensor_scalar(xn[:, t, :], X[:, n, :], mv[:, n, 0:1], rstd[:, n:n + 1],
                                                   ALU.subtract, ALU.mult)
                last.then_inc(ready, 1)

            def bank(n):
                return WB[:, n % NB, :]

            def split(high, low, src):
                step(nc.vector.tensor_copy(high, src))
                return nc.vector.tensor_tensor(low, src, high, ALU.subtract)

            def last_low(n):
                dve.wait_ge(s_last_high, n + 1)
                nc.vector.scalar_tensor_tensor(out=WE[:, NE - 1, 2 * n + 1, :], in0=part_stage(3 * NE - 3 + n),
                                               scalar=WSCALE, in1=WE[:, NE - 1, 2 * n, :],
                                               op0=ALU.mult, op1=ALU.subtract).then_inc(s_last_low, 1)

            def choose(b, src, n):
                if b:
                    dve.wait_ge(s_share, b)
                    dve.wait_ge(s_slot, b)
                first = nc.vector.tensor_scalar(lg[:, :, :].rearrange("p t e -> p (t e)"), src[:, 0:TT * NE],
                                                1.0 / WSCALE, None, ALU.mult)
                step(first)
                for t in range(TT):
                    last = nc.vector.max(m8[:, t, :], lg[:, t, :])
                step(last)
                nc.vector.tensor_tensor(gap[:, :], m8[:, :, 1], m8[:, :, 0], ALU.subtract).then_inc(s_gap, 1)
                for t in range(TT):
                    last = nc.vector.max_index(i8[:, t, :], m8[:, t, :], lg[:, t, :])
                step(last)
                step(nc.vector.tensor_copy(idf[:, :, :], i8[:, :, 0:2]))
                for k in range(2):
                    last = nc.vector.tensor_tensor(
                        pick[:, k, TT * b:TT * (b + 1), :], iota_e[:, :].rearrange("p (a e) -> p a e", a=1).broadcast_to([P, TT, NE]),
                        idf[:, :, k:k + 1].broadcast_to([P, TT, NE]), ALU.is_equal)
                step(last)
                return nc.vector.tensor_tensor(both[:, :, :], pick[:, 0, TT * b:TT * (b + 1), :],
                                               pick[:, 1, TT * b:TT * (b + 1), :], ALU.add)

            def weigh_choices(b):
                dve.wait_ge(s_egap, b + 1)
                step(nc.vector.tensor_scalar(den[:, :], egap[:, :], 1.0, None, ALU.add))
                step(nc.vector.reciprocal(den[:, :], den[:, :]))
                step(nc.vector.tensor_scalar(share[:, TT * b:TT * (b + 1), 0], den[:, :], tg[:, 1:2],
                                             1.0 / (WSCALE * WSCALE), ALU.mult, ALU.mult))
                nc.vector.tensor_tensor(share[:, TT * b:TT * (b + 1), 1], share[:, TT * b:TT * (b + 1), 0],
                                        egap[:, :], ALU.mult).then_inc(s_share, 1)

            def number_slots(b, src):
                ranks = src[:, 0:TT * NE].rearrange("p (t e) -> p t e", t=TT)
                step(nc.vector.tensor_tensor(slot_of[:, :, :], ranks, next_slot[:, :].rearrange(
                    "p (a e) -> p a e", a=1).broadcast_to([P, TT, NE]), ALU.add))
                for k in range(2):
                    step(nc.vector.tensor_tensor(chosen[:, :, :], slot_of[:, :, :],
                                                 pick[:, k, TT * b:TT * (b + 1), :], ALU.mult))
                    step(nc.vector.reduce_sum(slots_f[:, k, TT * b:TT * (b + 1)], chosen[:, :, :], AX_X))
                nc.vector.tensor_copy(slot[:, :, TT * b:TT * (b + 1)], slots_f[:, :, TT * b:TT * (b + 1)]).then_inc(s_slot, 1)
                dve.wait_ge(s_slot, b + 1)
                return nc.vector.tensor_tensor(next_slot[:, :], src[:, TT * NE:TT * NE + NE], next_slot[:, :], ALU.add)

            def list_tiles():
                emptied(dve, "rank", B - 1)
                one = slice(0, 1)
                step(nc.vector.scalar_tensor_tensor(out=cnt[:, :], in0=iota_e[:, :], scalar=-float(REGION),
                                                    in1=next_slot[:, :], op0=ALU.mult, op1=ALU.add))
                step(nc.vector.tensor_scalar(cnt_i[:, 0, :], cnt[:, :], float(P - 1), None, ALU.add))
                step(nc.vector.tensor_scalar(cnt_i[:, 1, :], cnt_i[:, 0, :], P.bit_length() - 1, None,
                                             ALU.logical_shift_right))
                step(nc.vector.tensor_copy(ntile[:, :], cnt_i[:, 1, :]))
                step(nc.vector.tensor_copy(cum[:, 0, :], ntile[:, :]))
                side, reach = 0, 1
                while reach < NE:
                    a, z = cum[:, side, :], cum[:, 1 - side, :]
                    nc.vector.tensor_copy(z[:, 0:reach], a[:, 0:reach])
                    step(nc.vector.tensor_tensor(z[:, reach:NE], a[:, reach:NE], a[:, 0:NE - reach], ALU.add))
                    side, reach = 1 - side, 2 * reach
                wide = [1, NT, NE - 1]
                step(nc.vector.tensor_tensor(
                    before[:, 0, :, :], cum[one, side, 0:NE - 1].rearrange("p (a e) -> p a e", a=1).broadcast_to(wide),
                    iota_t[:, :].rearrange("p (t a) -> p t a", a=1).broadcast_to(wide), ALU.is_le))
                step(nc.vector.tensor_tensor(
                    before[:, 1, :, :], before[:, 0, :, :],
                    ntile[one, 0:NE - 1].rearrange("p (a e) -> p a e", a=1).broadcast_to(wide), ALU.mult))
                step(nc.vector.reduce_sum(tile_f[:, 0:2, :], before[:, :, :, :], AX_X))
                nc.vector.tensor_copy(tile_e[:, :], tile_f[:, 0, :])
                step(nc.vector.tensor_tensor(tile_f[:, 2, :], iota_t[:, :], tile_f[:, 1, :], ALU.subtract))
                step(nc.vector.tensor_scalar(tile_f[:, 2, :], tile_f[:, 2, :], float(P), None, ALU.mult))
                nc.vector.scalar_tensor_tensor(out=tile_s[:, :], in0=tile_f[:, 0, :], scalar=float(REGION),
                                               in1=tile_f[:, 2, :], op0=ALU.mult, op1=ALU.add).then_inc(s_tiles, 1)
                step(nc.vector.tensor_tensor(shift[:, :], cum[:, side, :], ntile[:, :], ALU.subtract))
                step(nc.vector.tensor_scalar(shift[:, :], shift[:, :], float(P), None, ALU.mult))
                step(nc.vector.scalar_tensor_tensor(out=shift[:, :], in0=iota_e[:, :], scalar=-float(REGION),
                                                    in1=shift[:, :], op0=ALU.mult, op1=ALU.add))
                for k in range(2):
                    last = nc.vector.tensor_tensor(shifted[:, k, :, :], pick[:, k, :, :], shift[:, :].rearrange(
                        "p (a e) -> p a e", a=1).broadcast_to([P, TILES, NE]), ALU.mult)
                step(last)
                step(nc.vector.reduce_sum(back_f[:, :, :], shifted[:, :, :, :], AX_X))
                nc.vector.tensor_tensor(back[:, :, :], back_f[:, :, :], slots_f[:, :, :], ALU.add).then_inc(s_backrow, 1)

            nc.vector.memset(PV[:, :], 0.0).then_inc(s_pz, 1)
            dve.wait_ge(s_x0, 16)
            stats(0, TT, s_stats)
            dve.wait_ge(s_small, 16 * 6)
            nc.vector.tensor_scalar(bq_s[:, :, :], bq_s[:, :, :], WSCALE, None, ALU.mult).then_inc(s_dve, 1)
            steps[0] += 1
            dve.wait_ge(s_tanh, 1)
            step(nc.vector.tensor_scalar(tg16[:, :], tg[:, :], 1.0 / WSCALE, None, ALU.mult))
            nc.vector.tensor_scalar(bo_b[:, :], bo_b[:, :], tg[:, 0:1], None, ALU.mult).then_inc(s_bias, 1)
            inverse_deviation(0, TT, s_sqrt, 1)
            normalise(0, s_xn)
            dve.wait_ge(s_wh, 1)
            nc.vector.scalar_tensor_tensor(out=wl[:, :, :, :].rearrange("p a k n -> p (a k n)"),
                                           in0=stage[:, :, :, :].rearrange("p a k n -> p (a k n)"), scalar=WSCALE,
                                           in1=wh[:, :, :, :].rearrange("p a k n -> p (a k n)"),
                                           op0=ALU.mult, op1=ALU.subtract).then_inc(s_wl, 1)
            dve.wait_ge(s_gate, 16)
            step(nc.vector.tensor_scalar(gh[:, :, :], g32[:, :, :], WSCALE, None, ALU.mult))
            nc.vector.scalar_tensor_tensor(out=gl[:, :, :].rearrange("p k n -> p (k n)"),
                                           in0=g32[:, :, :].rearrange("p k n -> p (k n)"), scalar=WSCALE,
                                           in1=gh[:, :, :].rearrange("p k n -> p (k n)"),
                                           op0=ALU.mult, op1=ALU.subtract).then_inc(s_gsplit, 1)
            dve.wait_ge(s_const, 1)
            for n, u in enumerate(order):
                kind, b = u[0], u[1]
                if kind == "xt" and u[2] == 0 and b:
                    normalise(b, s_xn)
                if kind == "max" and u[2:] == (0, 0, 0) and b == 0:
                    dve.wait_ge(s_x, 16)
                    stats(TT, TILES, s_stats)
                    inverse_deviation(TT, TILES, s_sqrt, 2)
                if b == B - 1 and (kind, u[-1]) in (("at", 0), ("wo", 0), ("xt2", 0)):
                    last_low(("at", "wo", "xt2").index(kind))
                if kind == "xt2" and u[2] == 0:
                    inverse_deviation(TT * b, TT * (b + 1), s_sqrt2, b + 1)
                    normalise(b, s_xn2)
                dve.wait_ge(s_fill, n + 1)
                src = bank(n)
                if kind == "xt":
                    last = split(xth[:, u[2], :], xtl[:, u[2], :], src)
                elif kind in "qk":
                    t, c = "qk".index(kind), u[2]
                    if b and t == 1 and c == 0:
                        for g in range(NG):
                            dve.wait_ge(s_stack[g], 16 * 12 * b)
                    high, low = nat[:, t, 0, c, :], nat[:, t, 1, c, :]
                    step(nc.vector.tensor_scalar(high, src, bq_s[:, t, c:c + 1], None, ALU.add))
                    last = nc.vector.scalar_tensor_tensor(out=low, in0=src, scalar=bq_s[:, t, c:c + 1], in1=high,
                                                          op0=ALU.add, op1=ALU.subtract)
                elif kind == "v":
                    if b == 0:
                        dve.wait_ge(s_vone, 3)
                    if b >= 2 and u[2] == 0:
                        dve.wait_ge(s_pv, SLOTS * (b - 1))
                    for tt in range(2):
                        last = nc.vector.scalar_tensor_tensor(
                            out=V[:, b % 2, 2 * u[2] + tt, :, 0:DH],
                            in0=src[:, D * tt:D * (tt + 1)].rearrange("p (h d) -> p h d", h=H), scalar=1.0 / WSCALE,
                            in1=bv_b[:, :].rearrange("p (h d) -> p h d", h=H), op0=ALU.mult, op1=ALU.add)
                elif kind == "max":
                    _, _, g, tt, j = u
                    last = nc.vector.reduce_max(mx[:, g % 2, tt, (j % 2) * 2 + j // 2:(j % 2) * 2 + j // 2 + 1],
                                                src, AX_X)
                elif kind == "mt":
                    g = u[2]
                    if b:
                        dve.wait_ge(s_mrow[g], 32 * b)
                    last = nc.vector.tensor_scalar(mrow[:, g, :], WB[0:G, n % NB, :], 1.0 / MSCALE, None, ALU.mult)
                elif kind == "ot":
                    g = u[2]
                    o = src.rearrange("p (t j w) -> p t j w", t=TT, j=G)
                    if b and g == 0:
                        dve.wait_ge(s_fill, number["at", b - 1, 1] + 1)
                    if b or g:
                        emptied(dve, "ot", b - (g == 0), (g - 1) % NG)
                    step(nc.vector.reciprocal(rec[:, :, :], o[:, :, :, DH]))
                    last = nc.vector.tensor_tensor(
                        att[:, :, G * DH * g:G * DH * (g + 1)].rearrange("p t (j d) -> p t j d", j=G),
                        o[:, :, :, 0:DH],
                        rec[:, :, :].rearrange("p t (j a) -> p t j a", a=1).broadcast_to([P, TT, G, DH]), ALU.mult)
                elif kind == "at":
                    last = split(ath[:, u[2], :], atl[:, u[2], :], src)
                elif kind == "wo":
                    if u[2] == 0:
                        dve.wait_ge(s_xbo, b + 1)
                    rows = X[:, TT * b + 2 * u[2]:TT * b + 2 * u[2] + 2, :].rearrange("p t d -> p (t d)")
                    last = nc.vector.scalar_tensor_tensor(out=rows, in0=src, scalar=tg16[:, 0:1], in1=rows,
                                                          op0=ALU.mult, op1=ALU.add)
                elif kind == "xt2":
                    last = split(ath[:, u[2], :], atl[:, u[2], :], src)
                elif kind == "gate":
                    last = choose(b, src, n)
                elif kind == "rank":
                    weigh_choices(b)
                    last = number_slots(b, src)
                last.then_inc(s_free, 1)
                if kind == "wo" and u[2] == 1:
                    dve.wait_ge(s_free, n + 1)
                    stats(TT * b, TT * (b + 1), s_stats2)
            list_tiles()

            def tile_split(i, par):
                dve.wait_ge(s_tx, i + 1)
                if since(i, 2):
                    dve.wait_ge(s_h, i - 1)
                nc.vector.tensor_copy(xs[:, par, 0, :], TX[:, 0:D]).then_inc(s_xhigh, 1)
                dve.wait_ge(s_xhigh, i + 1)
                nc.vector.tensor_tensor(xs[:, par, 1, :], TX[:, 0:D], xs[:, par, 0, :], ALU.subtract).then_inc(s_xs, 1)

            def middle(i, par):
                dve.wait_ge(s_silu, i + 1)
                if since(i, 2):
                    dve.wait_ge(s_tm, i - 1)
                nc.vector.tensor_tensor(mid[:, par, :], HB[:, par, 1, :], silu[:, par, :], ALU.mult).then_inc(s_mid, 1)

            def middle_split(i, par):
                dve.wait_ge(s_tm, i + 1)
                if since(i, 2):
                    dve.wait_ge(s_y, i - 1)
                nc.vector.tensor_copy(ms[:, par, 0, :], TM).then_inc(s_mhigh, 1)
                dve.wait_ge(s_mhigh, i + 1)
                nc.vector.tensor_tensor(ms[:, par, 1, :], TM, ms[:, par, 0, :], ALU.subtract).then_inc(s_ms, 1)

            def expert_step(i, par):
                if not (isinstance(i, int) and i >= NT - 1):
                    tile_split(i + 1, 1 - par)
                if since(i, 1):
                    middle_split(i - 1, 1 - par)
                if not (isinstance(i, int) and i >= NT):
                    middle(i, par)

            tile_split(0, 0)
            for i in range(4):
                expert_step(i, i % 2)
            with dve.Fori(4, NT - 1, 2) as i:
                for o in range(2):
                    expert_step(i + o, o)
            for i in range(NT - 1, NT + 1):
                expert_step(i, i % 2)
            for t in range(TILES):
                if t % TT == 0:
                    dve.wait_ge(s_back[t // TT], 16 * 2 * TT)
                for k in range(2):
                    ins = nc.vector.scalar_tensor_tensor(out=X[:, t, :], in0=gy[:, t, k, :], scalar=share[:, t, k:k + 1],
                                                         in1=X[:, t, :], op0=ALU.mult, op1=ALU.add)
                    if k == 0:
                        step(ins)
                if t % TT == TT - 1:
                    ins.then_inc(s_sum, 1)

        @block.tensor
        def _(pe):
            count = [0]

            def three(dst, sh, sl, mh, ml, first, last):
                nc.tensor.matmul(dst, sh, mh, start=first, stop=False)
                nc.tensor.matmul(dst, sh, ml, start=False, stop=False)
                return nc.tensor.matmul(dst, sl, mh, start=False, stop=last)

            def unit(u):
                n = count[0]
                count[0] += 1
                assert order[n] == u
                kind, b = u[0], u[1]
                if n >= NB:
                    pe.wait_ge(s_free, n - NB + 1)
                dst = WB[:, n % NB, :]
                if kind == "xt":
                    pe.wait_ge(s_xn, b + 1)
                    for t in range(TT):
                        last = nc.tensor.transpose(dst[:, P * t:P * (t + 1)], xn[:, t, P * u[2]:P * (u[2] + 1)], ident[:, :])
                elif kind in "qk":
                    t, c = "qk".index(kind), u[2]
                    if kind == "q":
                        emptied(pe, "xt", b, 1)
                    else:
                        pe.wait_ge(s_ctsplit, b + 1)
                    mh, ml = ((xth, xtl), (cth, ctl))[t]
                    for k in range(KD):
                        last = three(dst, wh[:, t, k, P * c:P * (c + 1)], wl[:, t, k, P * c:P * (c + 1)],
                                     mh[:, k, :], ml[:, k, :], k == 0, k == KD - 1)
                elif kind == "v":
                    for tt in range(2):
                        tok = slice(P * (2 * u[2] + tt), P * (2 * u[2] + tt + 1))
                        for k in range(KD):
                            last = three(dst[:, D * tt:D * (tt + 1)], cth[:, k, tok], ctl[:, k, tok],
                                         wh[:, 2, k, :], wl[:, 2, k, :], k == 0, k == KD - 1)
                elif kind == "max":
                    _, _, g, tt, j = u
                    if (tt, j) == (0, 0):
                        pe.wait_ge(s_stack[g], 16 * 12 * (b + 1))
                    r, pair = j % 2, 2 * g + j // 2
                    last = nc.tensor.matmul(dst, QS[64 * r:64 * r + KS_ROWS, pair, P * tt:P * (tt + 1)],
                                            KS[64 * r:64 * r + KS_ROWS, pair, :], start=True, stop=True)
                elif kind == "mt":
                    g = u[2]
                    emptied(pe, "max", b, g, TT - 1, G - 1)
                    for t in range(TT):
                        last = nc.tensor.transpose(dst[0:G, P * t:P * (t + 1)], mx[:, g % 2, t, :], ident[:, :])
                elif kind == "ot":
                    q = NG * b + u[2]
                    pe.wait_ge(s_ot, q + 1)
                    for t in range(TT):
                        last = nc.tensor.transpose(dst[:, P * t:P * (t + 1)], OT[:, q % 2, P * t:P * (t + 1)], ident[:, :])
                elif kind == "at":
                    emptied(pe, "ot", b, NG - 1)
                    for t in range(TT):
                        last = nc.tensor.transpose(dst[:, P * t:P * (t + 1)], att[:, t, P * u[2]:P * (u[2] + 1)], ident[:, :])
                elif kind == "wo":
                    emptied(pe, "at", b, 1)
                    for tt in range(2):
                        tok = slice(P * (2 * u[2] + tt), P * (2 * u[2] + tt + 1))
                        for k in range(KD):
                            last = three(dst[:, D * tt:D * (tt + 1)], ath[:, k, tok], atl[:, k, tok],
                                         wh[:, 3, k, :], wl[:, 3, k, :], k == 0, k == KD - 1)
                elif kind == "xt2":
                    pe.wait_ge(s_xn2, b + 1)
                    for t in range(TT):
                        last = nc.tensor.transpose(dst[:, P * t:P * (t + 1)], xn[:, t, P * u[2]:P * (u[2] + 1)], ident[:, :])
                elif kind == "gate":
                    emptied(pe, "xt2", b, 1)
                    if b == 0:
                        pe.wait_ge(s_gsplit, 1)
                    for t in range(TT):
                        for k in range(KD):
                            last = three(dst[:, NE * t:NE * (t + 1)], ath[:, k, P * t:P * (t + 1)],
                                         atl[:, k, P * t:P * (t + 1)], gh[:, k, :], gl[:, k, :], k == 0, k == KD - 1)
                elif kind == "rank":
                    emptied(pe, "gate", b)
                    if b == 0:
                        pe.wait_ge(s_const, 1)
                    for t in range(TT + 1):
                        for a in range(min(t + 1, TT)):
                            last = nc.tensor.matmul(dst[:, NE * t:NE * (t + 1)], (earlier if a == t else ones)[:, :],
                                                    both[:, a, :], start=(a == 0), stop=(a == min(t, TT - 1)))
                last.then_inc(s_fill, 1)

            def scores(n):
                s, pp = divmod(n, 2)
                b, s = divmod(s, SLOTS)
                g, st = divmod(s, TT)
                if (st, pp) == (0, 0):
                    pe.wait_ge(s_mrow[g], 32 * (b + 1))
                if n >= 2:
                    pe.wait_ge(s_exp, n - 1)
                for r in range(2):
                    rows = slice(64 * r, 64 * r + KS_ROWS + 1)
                    last = nc.tensor.matmul(SC[:, n % 2, r, :], KS[rows, 2 * g + pp, P * st:P * (st + 1)],
                                            QS[rows, 2 * g + pp, :], start=True, stop=True)
                last.then_inc(s_score, 1)

            def weigh(s):
                b, q = divmod(s, SLOTS)
                g, st = divmod(q, TT)
                pe.wait_ge(s_exp, 2 * s + 2)
                if st == 0 and s:
                    pe.wait_ge(s_ot, s // TT)
                if st == 0 and g == 0:
                    emptied(pe, "v", b, 1)
                for j in range(G):
                    last = nc.tensor.matmul(PV[32 * j:32 * j + VW, :], V[:, b % 2, st, G * g + j, :],
                                            E[:, (2 * s + j // 2) % 4, j % 2, :], start=(st == 0), stop=(st == TT - 1))
                last.then_inc(s_pv, 1)

            pe.wait_ge(s_ident, 1)
            pe.wait_ge(s_wh, 1)
            pe.wait_ge(s_wl, 1)
            pe.wait_ge(s_vone, 3)
            pe.wait_ge(s_pz, 1)
            for u in slot_units[-1]:
                unit(u)
            scores(0)
            scores(1)
            for s in range(B * SLOTS):
                units = slot_units[s]
                for u in units[:len(units) // 2]:
                    unit(u)
                if s + 1 < B * SLOTS:
                    scores(2 * s + 2)
                for u in units[len(units) // 2:]:
                    unit(u)
                if s + 1 < B * SLOTS:
                    scores(2 * s + 3)
                weigh(s)
            for s in range(B * SLOTS, B * SLOTS + 12):
                for u in slot_units[s]:
                    unit(u)

            def turn_tile(i, par):
                pe.wait_ge(s_xg[par], i * 8 - 8 * par + 16)
                if since(i, 1):
                    pe.wait_ge(s_xs, i)
                for k in range(KD):
                    last = nc.tensor.transpose(TX[:, P * k:P * (k + 1)], xg[:, par, P * k:P * (k + 1)], ident[:, :])
                last.then_inc(s_tx, 1)

            def hidden(i, par, e):
                pe.wait_ge(s_xs, i + 1)
                if since(i, 2):
                    pe.wait_ge(s_mid, i - 1)
                for k in range(KD):
                    xh, xl = (xs[:, par, h, P * k:P * (k + 1)] for h in range(2))
                    for m in range(2):
                        high, low = (WE[:, bass.ds(e, 1), 2 * m + h, HID * k:HID * (k + 1)].rearrange(
                            "p a n -> p (a n)") for h in range(2))
                        last = three(HB[:, par, m, :], xh, xl, high, low, k == 0, k == KD - 1)
                last.then_inc(s_h, 1)

            def turn_middle(i, par):
                pe.wait_ge(s_mid, i + 1)
                if since(i, 1):
                    pe.wait_ge(s_ms, i)
                for k in range(KH):
                    last = nc.tensor.transpose(TM[:, P * k:P * (k + 1)], mid[:, par, P * k:P * (k + 1)], ident[:, :])
                last.then_inc(s_tm, 1)

            def output(i, par, e):
                pe.wait_ge(s_ms, i + 1)
                if since(i, 2):
                    pe.wait_ge(s_ysb, i - 1)
                for k in range(KH):
                    mh, ml = (ms[:, par, h, P * k:P * (k + 1)] for h in range(2))
                    high, low = (WE[:, bass.ds(e, 1), 4 + h, D * k:D * (k + 1)].rearrange(
                        "p a n -> p (a n)") for h in range(2))
                    last = three(YB[par][:, 0:D], mh, ml, high, low, k == 0, k == KH - 1)
                last.then_inc(s_y, 1)

            def expert(i):
                return pe.value_load(tile_e[0:1, bass.ds(i, 1)], min_val=0, max_val=NE - 1)

            pe.wait_ge(s_tiles, 1)
            pe.wait_ge(s_wsplit, 3 * (NE - 1))
            pe.wait_ge(s_last_low, 3)
            def expert_step(i, par):
                if not (isinstance(i, int) and i >= NT):
                    hidden(i, par, expert(i))
                if not (isinstance(i, int) and i >= NT - 1):
                    turn_tile(i + 1, 1 - par)
                if since(i, 1) and not (isinstance(i, int) and i > NT):
                    turn_middle(i - 1, 1 - par)
                if since(i, 2):
                    output(i - 2, par, expert(i - 2))

            turn_tile(0, 0)
            for i in range(4):
                expert_step(i, i % 2)
            with pe.Fori(4, NT - 1, 2) as i:
                for o in range(2):
                    expert_step(i + o, o)
            for i in range(NT - 1, NT + 2):
                expert_step(i, i % 2)


_NAMES = ["x", "ctxT", "g_xattn", "g_ffn", "wq", "bq", "wk", "bk", "wv", "bv", "woT", "bo", "gate", "w0", "w1", "wo"]


def kernel(x, ctx_1024, g_xattn, g_ffn, L0_xattn_Wq, L0_xattn_bq, L0_xattn_Wk, L0_xattn_bk, L0_xattn_Wv, L0_xattn_bv,
           L0_xattn_Wo, L0_xattn_bo, L0_ffn_gate_kernel, L0_ffn_w0_kernel, L0_ffn_w1_kernel, L0_ffn_wo_kernel):
    import numpy as np
    import concourse.bacc as bacc
    from concourse import mybir as mb
    from concourse.bass_utils import run_bass_kernel_spmd

    def packed(a):
        return np.ascontiguousarray(np.asarray(a))

    B, S, D = x.shape
    H, _, DH = L0_xattn_Wq.shape
    heads = [2 * (2 * (i // 2) + c) + i % 2 for c in range(2) for i in range(H // 2)]

    def columns(w, order):
        return packed(np.asarray(w)[order].transpose(1, 0, 2).reshape(D, H * DH))

    arrays = {
        "x": packed(x).reshape(B * S, D),
        "ctxT": packed(np.asarray(ctx_1024).transpose(0, 2, 1)),
        "g_xattn": packed(g_xattn), "g_ffn": packed(g_ffn),
        "wq": columns(L0_xattn_Wq, heads), "bq": packed(np.asarray(L0_xattn_bq)[heads].reshape(2, -1).T),
        "wk": columns(L0_xattn_Wk, heads), "bk": packed(np.asarray(L0_xattn_bk)[heads].reshape(2, -1).T),
        "wv": columns(L0_xattn_Wv, list(range(H))), "bv": packed(np.asarray(L0_xattn_bv).reshape(-1)),
        "woT": packed(np.asarray(L0_xattn_Wo).T), "bo": packed(L0_xattn_bo),
        "gate": packed(L0_ffn_gate_kernel),
        "w0": packed(L0_ffn_w0_kernel), "w1": packed(L0_ffn_w1_kernel), "wo": packed(L0_ffn_wo_kernel),
    }
    arrays["g_xattn"] = arrays["g_xattn"].reshape(-1)
    arrays["g_ffn"] = arrays["g_ffn"].reshape(-1)
    nc = bacc.Bacc("TRN2", target_bir_lowering=False, num_devices=1)
    aps = [nc.dram_tensor(f"in_{n}", arrays[n].shape, mb.dt.from_np(arrays[n].dtype), kind="ExternalInput").ap()
           for n in _NAMES]
    out = nc.dram_tensor("out", (B * S, D), mb.dt.float32, kind="ExternalOutput").ap()
    program(nc, *aps, out)
    r = run_bass_kernel_spmd(nc, [{f"in_{n}": arrays[n] for n in _NAMES}], core_ids=[0])
    return r.results[0]["out"].reshape(B, S, D)
```

```python
import concourse.bass as bass
from concourse import mybir
from contextlib import ExitStack

F32 = mybir.dt.float32
F16 = mybir.dt.float16
I32 = mybir.dt.int32
U32 = mybir.dt.uint32
ALU = mybir.AluOpType
ACT = mybir.ActivationFunctionType
AX_X = mybir.AxisListType.X

P = 128
EPS = 1e-5
WSCALE = 16.0
MSCALE = 256.0


def program(nc, x, ctxT, g_xattn, g_ffn, wq, bq, wk, bk, wv, bv, woT, bo, gate, w0, w1, wo, out):
    TOKENS, D = x.shape
    B, _, S = ctxT.shape
    KD = D // P
    TT = S // P
    TILES = TOKENS // P
    H = 16
    DH = D // H
    G = 4
    NG = H // G
    VW = DH + 1
    KS_ROWS = 3 * DH
    SLOTS = NG * TT
    _, NE = gate.shape
    HID = w0.shape[2]
    KH = HID // P
    REGION = TOKENS
    NT = (2 * TOKENS + NE * (P - 1)) // P
    SPARE = (NE - 1) * REGION + NT * P
    SCORE_SCALE = 1.0 / (float(DH) ** 0.5 * WSCALE * WSCALE)

    with ExitStack() as ctx:
        def sb(name, shape, dt):
            return ctx.enter_context(nc.sbuf_tensor(name, shape, dt))

        def psum(name, shape, dt=F32):
            return ctx.enter_context(nc.psum_tensor(name, shape, dt))

        def sem(name):
            return ctx.enter_context(nc.semaphore(name))

        ident = sb("ident", [P, P], F32)
        pad = sb("pad", [P, 1], F32)
        WE = sb("WE", [P, NE, 6, KD * HID], F16)
        last_expert = WE[:, NE - 1, :, :].rearrange("p a n -> p (a n)")
        X = sb("X", [P, TILES, D], F32)
        stage = sb("stage", [P, 4, KD, D], F32)
        wh = sb("wh", [P, 4, KD, D], F16)
        wl = sb("wl", [P, 4, KD, D], F16)
        bq_s = sb("bq_s", [P, 2, 2], F32)
        bv_b = sb("bv_b", [P, D], F32)
        bo_b = sb("bo_b", [P, D], F32)
        gains = sb("gains", [P, 2], F32)
        tg = sb("tg", [P, 2], F32)
        tg16 = sb("tg16", [P, 2], F32)
        st6 = sb("st6", [P, TILES, 6], F32)
        mv = sb("mv", [P, TILES, 2], F32)
        sd = sb("sd", [P, TILES], F32)
        nw = sb("nw", [P, 2, TILES], F32)
        rstd = sb("rstd", [P, TILES], F32)
        xn = sb("xn", [P, TT, D], F32)
        xth = sb("xth", [P, KD, S], F16)
        xtl = sb("xtl", [P, KD, S], F16)
        c32 = sb("c32", [P, KD, S], F32)
        cth = last_expert[:, 4096:5120].rearrange("p (k s) -> p k s", k=KD)
        ctl = last_expert[:, 5120:6144].rearrange("p (k s) -> p k s", k=KD)
        nat = sb("nat", [P, 2, 2, 2, S], F16)
        QS = last_expert[:, 0:4096].rearrange("p (h s) -> p h s", h=H // 2)
        KS = sb("KS", [P, H // 2, 2, S], F16)
        V = sb("V", [P, 2, TT, H, VW], F32)
        mx = sb("mx", [P, 2, TT, G], F32)
        mrow = sb("mrow", [G, NG, S], F16)
        E = sb("E", [P, 4, 2, S], F32)
        OT = sb("OT", [P, 2, S], F32)
        rec = sb("rec", [P, TT, G], F32)
        att = sb("att", [P, TT, D], F32)
        ath, atl = xth, xtl

        g32 = sb("g32", [P, KD, NE], F32)
        gh = sb("gh", [P, KD, NE], F16)
        gl = sb("gl", [P, KD, NE], F16)
        earlier = sb("earlier", [P, P], F16)
        ones = sb("ones", [P, P], F16)
        iota_e = sb("iota_e", [P, NE], F32)
        iota_t = sb("iota_t", [1, NT], F32)
        entry = sb("entry", [P, TILES, 2, 2], I32)
        weight = entry[:, :, :, 1].bitcast(F32)
        lg = sb("lg", [P, TT, NE], F32)
        m8 = sb("m8", [P, TT, 8], F32)
        i8 = sb("i8", [P, TT, 8], U32)
        idf = sb("idf", [P, TT, 2], F32)
        pick = sb("pick", [P, 2, TILES, NE], F32)
        both = sb("both", [P, TT, NE], F16)
        gap = sb("gap", [P, TT], F32)
        egap = sb("egap", [P, TT], F32)
        den = sb("den", [P, TT], F32)
        next_slot = sb("next_slot", [P, NE], F32)
        slot_of = sb("slot_of", [P, TT, NE], F32)
        chosen = sb("chosen", [P, TT, NE], F32)
        slot = sb("slot", [P, 2, TILES], I32)
        cnt = sb("cnt", [P, NE], F32)
        cnt_i = sb("cnt_i", [P, 2, NE], I32)
        ntile = sb("ntile", [P, NE], F32)
        cum = sb("cum", [P, 2, NE], F32)
        attf = att[:, :, :].rearrange("p t d -> p (t d)")
        before = attf[0:1, 0:2 * NT * (NE - 1)].rearrange("p (a t e) -> p a t e", a=2, t=NT)
        tile_f = attf[0:1, 2 * NT * (NE - 1):2 * NT * (NE - 1) + 3 * NT].rearrange("p (a t) -> p a t", a=3)
        tile_e = sb("tile_e", [1, NT], I32)
        tile_s = sb("tile_s", [1, NT], I32)
        slots_f = sb("slots_f", [P, 2, TILES], F32)
        Ef = E[:, :, :, :].rearrange("p a b n -> p (a b n)")
        xg = Ef[:, 0:512].rearrange("p (b d) -> p b d", b=2)
        silu = Ef[:, 512:1536].rearrange("p (b n) -> p b n", b=2)
        mid = Ef[:, 1536:2560].rearrange("p (b n) -> p b n", b=2)
        ysb = Ef[:, 2560:3072].rearrange("p (b n) -> p b n", b=2)
        natf = nat[:, :, :, :, :].rearrange("p a b c n -> p (a b c n)")
        xs = natf[:, 0:1024].rearrange("p (b h n) -> p b h n", b=2, h=2)
        ms = natf[:, 1024:3072].rearrange("p (b h n) -> p b h n", b=2, h=2)
        filled = Ef[:, 3072:3072 + 2 * NT].bitcast(I32).rearrange("p (t a) -> p t a", a=2)
        empty = Ef[:, 0:2 * (SPARE // P)].bitcast(I32).rearrange("p (n a) -> p n a", a=2)
        slot_no = Ef[:, 512:512 + SPARE // P].bitcast(I32)
        nil = Ef[:, 1024:1024 + D]
        rows_d = nc.dram_tensor("rows_by_token", (TOKENS + P, D), F32, kind="Internal").ap()
        slot_d = nc.dram_tensor("entry_by_slot", (SPARE, 2), I32, kind="Internal").ap()

        SC = psum("SC", [P, 2, 2, S])
        PV = psum("PV", [P, S])
        NB = 3
        WB = psum("WB", [P, NB, 512])
        HB = SC
        TX, TM, YB = WB[:, 0, :], WB[:, 1, :], (WB[:, 2, :], PV)

        s_x0 = sem("x_first_batch_loaded")
        s_x = sem("x_other_batches_loaded")
        s_wk = sem("key_weights_loaded")
        s_wq = sem("query_weights_loaded")
        s_w2 = sem("value_and_output_weights_loaded")
        s_qkbias = sem("query_and_key_biases_loaded")
        s_small = sem("other_biases_and_gains_loaded")
        s_ctx = sem("context_loaded")
        s_ident = sem("identity_made")
        s_vone = sem("value_ones_set")
        s_qpad = sem("query_rows_padded")
        s_pad = sem("zero_made")
        s_kpad = sem("key_rows_padded")
        s_zpad = sem("other_heads_rows_cleared")
        s_wh = sem("weight_high_parts_made")
        s_wl = sem("weight_low_parts_made")
        s_ctsplit = sem("context_split")
        s_bias = sem("biases_scaled")
        s_tanh = sem("gains_tanh_made")
        s_stats = sem("variances_ready")
        s_sqrt = sem("deviations_ready")
        s_xn = sem("rows_normalised")
        s_xbo = sem("output_bias_added")
        s_fill = sem("work_bank_filled")
        s_free = sem("work_bank_emptied")
        s_dve = sem("vector_step_done")
        s_pool = sem("pool_step_done")
        s_stack = [sem(f"group{g}_stacked") for g in range(NG)]
        s_mrow = [sem(f"group{g}_maxima_placed") for g in range(NG)]
        s_score = sem("scores_done")
        s_exp = sem("exponentials_done")
        s_pv = sem("values_weighted")
        s_ot = sem("attention_output_copied")
        s_pz = sem("output_bank_zeroed")
        s_gate = sem("router_weights_loaded")
        s_gsplit = sem("router_weights_split")
        s_slotno = sem("slot_numbers_made")
        s_const = sem("router_constants_made")
        s_zero = sem("token_table_cleared")
        s_rows = sem("rows_stored")
        s_gap = sem("choice_gaps_ready")
        s_egap = sem("choice_gaps_exponentiated")
        s_xhigh = sem("tile_high_part_made")
        s_mhigh = sem("middle_high_part_made")
        s_stats2 = sem("expert_input_variances_ready")
        s_sqrt2 = sem("expert_input_deviations_ready")
        s_xn2 = sem("expert_input_normalised")
        s_share = sem("choices_weighed")
        s_slot = sem("slots_numbered")
        s_idput = sem("tokens_placed")
        s_tiles = sem("tiles_listed")
        s_we = [sem(f"expert_weights_loaded{i}") for i in range(2)]
        s_whigh = sem("expert_weight_high_parts_made")
        s_w16 = sem("expert_weights_scaled")
        s_cth = sem("context_high_parts_made")
        s_empty = sem("empty_entries_made")
        s_wsplit = sem("expert_weights_split")
        s_last_high = sem("last_expert_high_parts_made")
        s_last_low = sem("last_expert_low_parts_made")
        NL = 4
        s_ids = [sem(f"tile_entries_loaded{i}") for i in range(NL)]
        s_xg = [sem(f"tile_rows_gathered{i}") for i in range(2)]
        s_tx = sem("tile_turned")
        s_xs = sem("tile_split")
        s_h = sem("hidden_sums_done")
        s_silu = sem("silu_done")
        s_mid = sem("middle_done")
        s_tm = sem("middle_turned")
        s_ms = sem("middle_split")
        s_y = sem("expert_output_done")
        s_ysb = sem("expert_output_copied")
        s_base = sem("attention_result_stored")
        s_add = sem("expert_output_added")

        slot_units = {s: [] for s in range(-1, B * SLOTS + 12)}

        def place(s, *unit):
            slot_units[s].append(unit)

        for b in range(B):
            base = SLOTS * (b - 1)
            at = (lambda o: -1) if b == 0 else (lambda o: base + o)
            for k in range(KD):
                place(at(0 + k), "xt", b, k)
            if b == 0:
                for c in range(2):
                    place(-1, "k", b, c)
            for c in range(2):
                if b:
                    place(at(2 + c), "k", b, c)
                place(at(2 + c), "q", b, c)
            for h in range(2):
                place(at(4 + h), "v", b, h)
        early = {(0, 0): (-1, -1), (0, 1): (0, 2), (0, 2): (2, 5), (0, 3): (5, 8)}
        for b in range(B):
            for g in range(NG):
                home = SLOTS * b + 4 * g
                first, last = early.get((b, g), (home - 10, home - 7))
                for n in range(TT * G):
                    place(first + (last - first + 1) * n // (TT * G), "max", b, g, n // G, n % G)
                place(last, "mt", b, g)
                place(home + 5, "ot", b, g)
        for b in range(B):
            end = SLOTS * (b + 1)
            for c in range(2):
                place(end + 4, "at", b, c)
            for h in range(2):
                place(end + 5, "wo", b, h)
            for k in range(KD):
                place(end + 7, "xt2", b, k)
            place(end + 8, "gate", b)
            place(end + 10, "rank", b)
        order = [u for s in sorted(slot_units) for u in slot_units[s]]
        number = {u: n for n, u in enumerate(order)}

        def emptied(eng, *unit):
            eng.wait_ge(s_free, number[unit] + 1)

        def part_slot(n):
            return 3 * n + 1

        def context_slot(b):
            return SLOTS * (b - 2) + 7

        def since(i, first):
            return not isinstance(i, int) or i >= first

        def part_stage(n):
            return stage[:, 2 * (n % 2):2 * (n % 2) + 2, :, :].rearrange("p a k n -> p (a k n)")

        block = ctx.enter_context(nc.Block())

        @block.sync
        def _(sp):
            xr = x.rearrange("(t p) d -> p t d", p=P)
            sp.dma_start(stage[:, 1, :, :], wk.rearrange("(k p) n -> p k n", p=P)).then_inc(s_wk, 16)
            sp.dma_start(X[:, 0:TT, :], xr[:, 0:TT, :]).then_inc(s_x0, 16)
            sp.dma_start(stage[:, 0, :, :], wq.rearrange("(k p) n -> p k n", p=P)).then_inc(s_wq, 16)
            for n, v in enumerate((bq, bk)):
                sp.dma_start(bq_s[:, n, :], v).then_inc(s_qkbias, 16)
            for n, w in ((2, wv), (3, woT)):
                sp.dma_start(stage[:, n, :, :], w.rearrange("(k p) n -> p k n", p=P)).then_inc(s_w2, 16)
            sp.dma_start(X[:, TT:TILES, :], xr[:, TT:TILES, :]).then_inc(s_x, 16)
            for t, v in ((bv_b, bv), (bo_b, bo)):
                sp.dma_start(t[:, :], v.rearrange("(a n) -> a n", a=1).broadcast_to([P, D])).then_inc(s_small, 16)
            sp.dma_start(g32[:, :, :], gate.rearrange("(k p) n -> p k n", p=P)).then_inc(s_gate, 16)
            for n, v in enumerate((g_xattn, g_ffn)):
                sp.dma_start(gains[:, n:n + 1], v.rearrange("(a n) -> a n", a=1).broadcast_to([P, 1])).then_inc(s_small, 16)

            def stack(t, b, g):
                if b:
                    sp.wait_ge(s_score, 2 * (SLOTS * (b - 1) + TT * (g + 1)))
                elif g == 0:
                    sp.wait_ge(*(s_qpad, 2) if t == 0 else (s_kpad, 2))
                    sp.wait_ge(s_zpad, 2)
                if g == 0:
                    emptied(sp, "qk"[t], b, 1)
                for r in range(2):
                    i = 2 * g + r
                    for o, part in enumerate(((0, 0, 1), (0, 1, 0))[t]):
                        rows = slice(64 * r + DH * o, 64 * r + DH * (o + 1))
                        to = QS[rows, 2 * g:2 * g + 2, :] if t == 0 else KS[rows, 2 * g:2 * g + 2, r, :]
                        sp.dma_start(to, nat[DH * i:DH * i + DH, t, part, :, :]).then_inc(s_stack[g], 16)

            def stack_keys(b, g):
                stack(1, b, g)

            def stack_queries(b, g):
                stack(0, b, g)

            def maxima(b, g):
                emptied(sp, "mt", b, g)
                for r in range(2):
                    row = 64 * r + KS_ROWS
                    sp.dma_start(QS[row:row + 1, 2 * g:2 * g + 2, :],
                                 mrow[2 * r:2 * r + 2, g, :]).then_inc(s_mrow[g], 16)

            def store_rows(b, g):
                sp.wait_ge(s_xn2, b + 1)
                sp.dma_start(rows_d[0:TOKENS, :].rearrange("(t p) d -> p t d", p=P)[:, TT * b:TT * (b + 1), :],
                             xn[:, :, :]).then_inc(s_rows, 16)

            def clear(b, g):
                sp.wait_ge(s_empty, 1)
                sp.wait_ge(s_const, 1)
                sp.dma_start(slot_d.rearrange("(p n) a -> p n a", p=P), empty).then_inc(s_zero, 16)
                sp.dma_start(rows_d[TOKENS:TOKENS + P, :], nil).then_inc(s_zero, 16)
                sp.dma_start(out[TOKENS:TOKENS + P, :], nil).then_inc(s_zero, 16)

            def store_base(b, g):
                emptied(sp, "wo", b, 1)
                sp.dma_start(out[0:TOKENS, :].rearrange("(t p) d -> p t d", p=P)[:, TT * b:TT * (b + 1), :],
                             X[:, TT * b:TT * (b + 1), :]).then_inc(s_base, 16)

            jobs = [(-4.5, 3, clear, 0, 0)]
            for b in range(B):
                jobs.append((SLOTS * (b + 1) + 7, 2, store_rows, b, 0))
                jobs.append((SLOTS * (b + 1) + 8, 3, store_base, b, 0))
                for g in range(NG):
                    home = SLOTS * b + 4 * g
                    jobs.append((home - 12 if b else g - NG - 2, 0, stack_keys, b, g))
                    jobs.append((home - 12 if b else g - NG - 2, 0.5, stack_queries, b, g))
                    jobs.append((early.get((b, g), (0, home - 7))[1] if b or g else -3.5, 1, maxima, b, g))
            for _, _, job, b, g in sorted(jobs, key=lambda j: (j[0], j[1], j[3], j[4])):
                job(b, g)

            def load_entries(i, lane):
                at = sp.value_load(tile_s[0:1, bass.ds(i, 1)], min_val=0, max_val=SPARE - P)
                if since(i, NL):
                    sp.wait_ge(s_ids[lane], (i - lane) * (16 // NL))
                sp.dma_start(filled[:, bass.ds(i, 1), :], slot_d[bass.ds(at, P), :].rearrange(
                    "p (a c) -> p a c", a=1)).then_inc(s_ids[lane], 16)

            sp.wait_ge(s_idput, 16 * 2 * TILES)
            sp.wait_ge(s_tiles, 1)
            for i in range(NL):
                load_entries(i, i)
            whole = NT // NL * NL
            with sp.Fori(NL, whole, NL) as i:
                for lane in range(NL):
                    load_entries(i + lane, lane)
            for i in range(whole, NT):
                load_entries(i, i % NL)
            sp.wait_ge(s_base, 16 * B)
            sp.wait_ge(s_add, 16 * NT)

        @block.gpsimd
        def _(pool):
            steps = [0]

            def step(ins):
                steps[0] += 1
                ins.then_inc(s_pool, 1)
                pool.wait_ge(s_pool, steps[0])

            pool.dma_start(c32[:, :, :], ctxT[0].rearrange("(k p) s -> p k s", p=P)).then_inc(s_ctx, 16)
            nc.gpsimd.memset(pad[:, :], 0.0).then_inc(s_pad, 1)
            step(nc.gpsimd.memset(ident[:, :], 0.0))
            nc.gpsimd.affine_select(out=ident[:, :], in_=ident[:, :], compare_op=ALU.not_equal, fill=1.0,
                                    base=0, pattern=[[-1, P]], channel_multiplier=1).then_inc(s_ident, 1)
            pool.wait_ge(s_ident, 1)

            def pad_keys(r):
                nc.gpsimd.memset(KS[64 * r + 32:64 * r + 64, :, r, :], -MSCALE).then_inc(s_kpad, 1)
                pool.wait_ge(s_kpad, r + 1)

            def constants():
                step(nc.gpsimd.memset(ones[:, :], 1.0))
                step(nc.gpsimd.memset(earlier[:, :], 1.0))
                step(nc.gpsimd.affine_select(out=earlier[:, :], in_=earlier[:, :], compare_op=ALU.is_gt, fill=0.0,
                                             base=0, pattern=[[1, P]], channel_multiplier=-1))
                step(nc.gpsimd.iota(iota_e[:, :], pattern=[[1, NE]], base=0, channel_multiplier=0,
                                    allow_small_or_imprecise_dtypes=True))
                step(nc.gpsimd.iota(iota_t[:, :], pattern=[[1, NT]], base=0, channel_multiplier=0,
                                    allow_small_or_imprecise_dtypes=True))
                step(nc.gpsimd.iota(next_slot[:, :], pattern=[[REGION, NE]], base=0, channel_multiplier=0,
                                    allow_small_or_imprecise_dtypes=True))
                nc.gpsimd.iota(entry[:, :, :, 0], pattern=[[P, TILES], [0, 2]], base=0,
                               channel_multiplier=1).then_inc(s_const, 1)

            def load_part(n):
                e, m = divmod(n, 3)
                src = (w0, w1, wo)[m][e]
                pool.dma_start(part_stage(n).rearrange("p (k n) -> p k n", n=src.shape[1]),
                               src.rearrange("(k p) n -> p k n", p=P)).then_inc(s_we[n % 2], 16)

            def low_part(n):
                e, m = divmod(n, 3)
                if n == 0:
                    pool.wait_ge(s_wl, 3)
                    load_part(0)
                    load_part(1)
                pool.wait_ge(s_w16, n + 1)
                nc.gpsimd.tensor_tensor(WE[:, e, 2 * m + 1, :], part_stage(n), WE[:, e, 2 * m, :],
                                        ALU.subtract).then_inc(s_wsplit, 1)
                pool.wait_ge(s_wsplit, n + 1)
                load_part(n + 2)

            def low_context(b):
                pool.wait_ge(s_cth, b + 1)
                nc.gpsimd.tensor_tensor(ctl[:, :, :], c32[:, :, :], cth[:, :, :], ALU.subtract).then_inc(s_ctsplit, 1)
                if b + 1 < B:
                    pool.wait_ge(s_ctsplit, b + 1)
                    pool.dma_start(c32[:, :, :], ctxT[b + 1].rearrange("(k p) s -> p k s", p=P)).then_inc(s_ctx, 16)

            def output_bias(b):
                pool.wait_ge(s_xn, b + 1)
                if b == 0:
                    pool.wait_ge(s_bias, 1)
                rows = X[:, TT * b:TT * (b + 1), :]
                nc.gpsimd.tensor_tensor(rows, rows, bo_b[:, :].rearrange("p (a d) -> p a d", a=1).broadcast_to([P, TT, D]),
                                        ALU.add).then_inc(s_xbo, 1)

            def place_entries(b):
                pool.wait_ge(s_slot, b + 1)
                if b == 0:
                    pool.wait_ge(s_zero, 16 * 3)
                for t in range(TT * b, TT * (b + 1)):
                    for k in range(2):
                        pool.indirect_dma_start(slot_d[:, :], bass.IndirectOffsetOnAxis(slot[:, k, t:t + 1].bitcast(U32), 0),
                                                entry[:, t, k, :], None).then_inc(s_idput, 16)

            pad_keys(0)
            low_context(0)
            pad_keys(1)
            nc.gpsimd.memset(V[:, :, :, :, :], 1.0).then_inc(s_vone, 1)
            pool.wait_ge(s_vone, 1)
            step(nc.gpsimd.memset(nil, 0.0))
            step(nc.gpsimd.memset(empty, 0))
            nc.gpsimd.iota(slot_no, pattern=[[1, SPARE // P]], base=0, channel_multiplier=SPARE // P).then_inc(s_slotno, 1)
            constants()
            jobs = [(part_slot(n), 0, low_part, n) for n in range(3 * (NE - 1))]
            for b in range(B):
                if b:
                    jobs.append((context_slot(b), 1, low_context, b))
                jobs.append((SLOTS * (b - 1) + 3, 2, output_bias, b))
                if b < B - 1:
                    jobs.append((SLOTS * (b + 1) + 11, 3, place_entries, b))
            for _, _, job, arg in sorted(jobs, key=lambda j: j[0:2]):
                job(arg)
            pool.wait_ge(s_last_low, 1)
            load_part(3 * NE - 1)
            place_entries(B - 1)

            def gather(i):
                pool.wait_ge(s_ids[i % NL], 16 * (i // NL + 1))
                if i >= 2:
                    pool.wait_ge(s_tx, i - 1)
                pool.indirect_dma_start(xg[:, i % 2, :], None, rows_d[:, :], bass.IndirectOffsetOnAxis(
                    filled[:, i, 0:1].bitcast(U32), 0)).then_inc(s_xg[i % 2], 16)

            def scatter(i):
                pool.wait_ge(s_ysb, i + 1)
                if i:
                    pool.wait_ge(s_add, 16 * i)
                pool.indirect_dma_start(out[:, :], bass.IndirectOffsetOnAxis(filled[:, i, 0:1].bitcast(U32), 0),
                                        ysb[:, i % 2, :], None, compute_op=ALU.add).then_inc(s_add, 16)

            pool.wait_ge(s_rows, 16 * B)
            pool.wait_ge(s_base, 16 * B)
            pool.wait_ge(s_pv, B * SLOTS)
            LAG = 6
            for i in range(NT + LAG):
                if i < NT:
                    gather(i)
                if i >= LAG:
                    scatter(i - LAG)

        @block.scalar
        def _(act):
            def copy_output(act, q):
                act.wait_ge(s_pv, TT * (q + 1))
                if q >= 2:
                    emptied(act, "ot", (q - 2) // NG, (q - 2) % NG)
                nc.scalar.activation(OT[:, q % 2, :], PV[:, :], ACT.Copy).then_inc(s_ot, 1)

            def second_norm(b):
                act.wait_ge(s_stats2, b + 1)
                nc.scalar.activation(sd[:, TT * b:TT * (b + 1)], nw[:, 0, TT * b:TT * (b + 1)], ACT.Sqrt).then_inc(s_sqrt2, 1)

            def choice_exp(b):
                act.wait_ge(s_gap, b + 1)
                nc.scalar.activation(egap[:, :], gap[:, :], ACT.Exp).then_inc(s_egap, 1)

            def high_context(b):
                act.wait_ge(s_ctx, 16 * (b + 1))
                if b:
                    emptied(act, "v", b - 1, 1)
                nc.scalar.activation(cth[:, :, :], c32[:, :, :], ACT.Copy).then_inc(s_cth, 1)

            def high_part(n):
                e, m = divmod(n, 3)
                act.wait_ge(s_we[n % 2], 16 * (n // 2 + 1))
                nc.scalar.activation(WE[:, e, 2 * m, :], part_stage(n), ACT.Copy, scale=WSCALE).then_inc(s_whigh, 1)
                act.wait_ge(s_whigh, n + 1)
                nc.scalar.activation(part_stage(n), part_stage(n), ACT.Copy, scale=WSCALE).then_inc(s_w16, 1)

            def other_head_rows(r):
                if r == 0:
                    act.wait_ge(s_pad, 1)
                rows = slice(64 * (1 - r), 64 * (2 - r))
                nc.scalar.activation(KS[rows, :, r, :], pad[rows, 0:1].rearrange("p (a n) -> p a n", a=1).broadcast_to(
                    [64, H // 2, S]), ACT.Copy).then_inc(s_zpad, 1)

            other_head_rows(0)
            for n, t, loaded in ((0, 1, s_wk), (1, 0, s_wq)):
                act.wait_ge(loaded, 16)
                nc.scalar.activation(wh[:, t, :, :], stage[:, t, :, :], ACT.Copy, scale=WSCALE).then_inc(s_wh, 1)
                if n == 0:
                    high_context(0)
            for n, (lo, hi) in enumerate(((0, TT), (TT, TILES))):
                act.wait_ge(s_stats, hi // TT)
                nc.scalar.activation(sd[:, lo:hi], nw[:, 0, lo:hi], ACT.Sqrt).then_inc(s_sqrt, 1)
                if n == 0:
                    other_head_rows(1)
                    act.wait_ge(s_w2, 16 * 2)
                    nc.scalar.activation(wh[:, 2:4, :, :], stage[:, 2:4, :, :], ACT.Copy, scale=WSCALE).then_inc(s_wh, 1)
                    act.wait_ge(s_small, 16 * 4)
                    nc.scalar.activation(tg[:, :], gains[:, :], ACT.Tanh).then_inc(s_tanh, 1)
            high_context(1)
            act.wait_ge(s_zero, 16 * 3)
            parts = {part_slot(n): n for n in range(3 * (NE - 1))}
            contexts = {context_slot(b): b for b in range(2, B)}
            for n in range(2 * B * SLOTS):
                act.wait_ge(s_score, n + 1)
                if n >= 4:
                    act.wait_ge(s_pv, (n - 4) // 2 + 1)
                nc.scalar.activation(E[:, n % 4, :, :], SC[:, n % 2, :, :], ACT.Exp,
                                     scale=SCORE_SCALE).then_inc(s_exp, 1)
                s, half = divmod(n, 2)
                if half == 1 and s % TT == 0 and s:
                    copy_output(act, s // TT - 1)
                if half == 1 and s in contexts:
                    high_context(contexts[s])
                if half == 1 and s in parts:
                    high_part(parts[s])
                if half == 1 and s >= SLOTS and s % SLOTS == 6:
                    second_norm(s // SLOTS - 1)
                if half == 1 and s >= SLOTS and s % SLOTS == 9:
                    choice_exp(s // SLOTS - 1)
            copy_output(act, B * NG - 1)
            for n in range(3):
                act.wait_ge(s_we[(3 * NE - 3 + n) % 2], 16 * ((3 * NE - 3 + n) // 2 + 1))
                if n == 0:
                    emptied(act, "v", B - 1, 1)
                nc.scalar.activation(WE[:, NE - 1, 2 * n, :], part_stage(3 * NE - 3 + n), ACT.Copy,
                                     scale=WSCALE).then_inc(s_last_high, 1)
            second_norm(B - 1)
            choice_exp(B - 1)

            def hidden(i, par):
                act.wait_ge(s_h, i + 1)
                if since(i, 2):
                    act.wait_ge(s_mid, i - 1)
                nc.scalar.activation(silu[:, par, :], HB[:, par, 0, :], ACT.Silu, scale=1.0 / WSCALE).then_inc(s_silu, 1)

            def output(i, par):
                act.wait_ge(s_y, i + 1)
                if since(i, 2):
                    act.wait_ge(s_add, i * 16 - 16)
                nc.scalar.activation(ysb[:, par, :], YB[par][:, 0:D], ACT.Copy,
                                     scale=filled[:, bass.ds(i, 1), 1].bitcast(F32)).then_inc(s_ysb, 1)

            def expert_step(i, par):
                if not (isinstance(i, int) and i >= NT):
                    hidden(i, par)
                if since(i, 2):
                    output(i - 2, par)

            for i in range(4):
                expert_step(i, i % 2)
            with act.Fori(4, NT - 1, 2) as i:
                for o in range(2):
                    expert_step(i + o, o)
            for i in range(NT - 1, NT + 2):
                expert_step(i, i % 2)

        @block.vector
        def _(dve):
            steps = [0]

            def step(ins):
                steps[0] += 1
                ins.then_inc(s_dve, 1)
                dve.wait_ge(s_dve, steps[0])

            def stats(lo, hi, ready):
                for t in range(lo, hi):
                    last = nc.vector.bn_stats(st6[:, t, :], X[:, t, :])
                step(last)
                for t in range(lo, hi):
                    last = nc.vector.bn_aggr(mv[:, t, :], st6[:, t, :])
                step(last)
                nc.vector.tensor_scalar(nw[:, 0, lo:hi], mv[:, lo:hi, 1], EPS, None, ALU.add).then_inc(ready, 1)

            def inverse_deviation(lo, hi, s_root, n):
                dve.wait_ge(s_root, n)
                v, a, r = nw[:, 0, lo:hi], nw[:, 1, lo:hi], rstd[:, lo:hi]
                step(nc.vector.reciprocal(r, sd[:, lo:hi]))
                step(nc.vector.tensor_tensor(a, r, r, ALU.mult))
                step(nc.vector.tensor_tensor(a, a, v, ALU.mult))
                step(nc.vector.tensor_scalar(a, a, -0.5, 1.5, ALU.mult, ALU.add))
                step(nc.vector.tensor_tensor(r, r, a, ALU.mult))

            def normalise(b, ready):
                if ready is s_xn2:
                    dve.wait_ge(s_fill, number["xt", min(b + 2, B - 1), 1] + 1)
                    stored = b
                else:
                    if b:
                        dve.wait_ge(s_fill, number["xt", b - 1, 1] + 1)
                    stored = b - 2
                if stored > 0:
                    dve.wait_ge(s_fill, number["xt2", stored - 1, 1] + 1)
                    dve.wait_ge(s_rows, 16 * stored)
                for t in range(TT):
                    n = TT * b + t
                    last = nc.vector.tensor_scalar(xn[:, t, :], X[:, n, :], mv[:, n, 0:1], rstd[:, n:n + 1],
                                                   ALU.subtract, ALU.mult)
                last.then_inc(ready, 1)

            def bank(n):
                return WB[:, n % NB, :]

            def split(high, low, src):
                step(nc.vector.tensor_copy(high, src))
                return nc.vector.tensor_tensor(low, src, high, ALU.subtract)

            def low_weights(which, n):
                dve.wait_ge(s_wh, n)
                nc.vector.scalar_tensor_tensor(out=wl[:, which, :, :].rearrange("p a k n -> p (a k n)"),
                                               in0=stage[:, which, :, :].rearrange("p a k n -> p (a k n)"), scalar=WSCALE,
                                               in1=wh[:, which, :, :].rearrange("p a k n -> p (a k n)"),
                                               op0=ALU.mult, op1=ALU.subtract).then_inc(s_wl, 1)

            def last_low(n):
                dve.wait_ge(s_last_high, n + 1)
                nc.vector.scalar_tensor_tensor(out=WE[:, NE - 1, 2 * n + 1, :], in0=part_stage(3 * NE - 3 + n),
                                               scalar=WSCALE, in1=WE[:, NE - 1, 2 * n, :],
                                               op0=ALU.mult, op1=ALU.subtract).then_inc(s_last_low, 1)

            def choose(b, src, n):
                if b:
                    dve.wait_ge(s_share, b)
                    dve.wait_ge(s_slot, b)
                first = nc.vector.tensor_scalar(lg[:, :, :].rearrange("p t e -> p (t e)"), src[:, 0:TT * NE],
                                                1.0 / WSCALE, None, ALU.mult)
                step(first)
                for t in range(TT):
                    last = nc.vector.max(m8[:, t, :], lg[:, t, :])
                step(last)
                nc.vector.tensor_tensor(gap[:, :], m8[:, :, 1], m8[:, :, 0], ALU.subtract).then_inc(s_gap, 1)
                for t in range(TT):
                    last = nc.vector.max_index(i8[:, t, :], m8[:, t, :], lg[:, t, :])
                step(last)
                step(nc.vector.tensor_copy(idf[:, :, :], i8[:, :, 0:2]))
                for k in range(2):
                    last = nc.vector.tensor_tensor(
                        pick[:, k, TT * b:TT * (b + 1), :], iota_e[:, :].rearrange("p (a e) -> p a e", a=1).broadcast_to([P, TT, NE]),
                        idf[:, :, k:k + 1].broadcast_to([P, TT, NE]), ALU.is_equal)
                step(last)
                return nc.vector.tensor_tensor(both[:, :, :], pick[:, 0, TT * b:TT * (b + 1), :],
                                               pick[:, 1, TT * b:TT * (b + 1), :], ALU.add)

            def weigh_choices(b):
                dve.wait_ge(s_egap, b + 1)
                step(nc.vector.tensor_scalar(den[:, :], egap[:, :], 1.0, None, ALU.add))
                step(nc.vector.reciprocal(den[:, :], den[:, :]))
                step(nc.vector.tensor_scalar(weight[:, TT * b:TT * (b + 1), 0], den[:, :], tg[:, 1:2],
                                             1.0 / (WSCALE * WSCALE), ALU.mult, ALU.mult))
                nc.vector.tensor_tensor(weight[:, TT * b:TT * (b + 1), 1], weight[:, TT * b:TT * (b + 1), 0],
                                        egap[:, :], ALU.mult).then_inc(s_share, 1)

            def number_slots(b, src):
                ranks = src[:, 0:TT * NE].rearrange("p (t e) -> p t e", t=TT)
                step(nc.vector.tensor_tensor(slot_of[:, :, :], ranks, next_slot[:, :].rearrange(
                    "p (a e) -> p a e", a=1).broadcast_to([P, TT, NE]), ALU.add))
                for k in range(2):
                    step(nc.vector.tensor_tensor(chosen[:, :, :], slot_of[:, :, :],
                                                 pick[:, k, TT * b:TT * (b + 1), :], ALU.mult))
                    step(nc.vector.reduce_sum(slots_f[:, k, TT * b:TT * (b + 1)], chosen[:, :, :], AX_X))
                nc.vector.tensor_copy(slot[:, :, TT * b:TT * (b + 1)], slots_f[:, :, TT * b:TT * (b + 1)]).then_inc(s_slot, 1)
                dve.wait_ge(s_slot, b + 1)
                return nc.vector.tensor_tensor(next_slot[:, :], src[:, TT * NE:TT * NE + NE], next_slot[:, :], ALU.add)

            def list_tiles():
                emptied(dve, "rank", B - 1)
                one = slice(0, 1)
                step(nc.vector.scalar_tensor_tensor(out=cnt[:, :], in0=iota_e[:, :], scalar=-float(REGION),
                                                    in1=next_slot[:, :], op0=ALU.mult, op1=ALU.add))
                step(nc.vector.tensor_scalar(cnt_i[:, 0, :], cnt[:, :], float(P - 1), None, ALU.add))
                step(nc.vector.tensor_scalar(cnt_i[:, 1, :], cnt_i[:, 0, :], P.bit_length() - 1, None,
                                             ALU.logical_shift_right))
                step(nc.vector.tensor_copy(ntile[:, :], cnt_i[:, 1, :]))
                step(nc.vector.tensor_copy(cum[:, 0, :], ntile[:, :]))
                side, reach = 0, 1
                while reach < NE:
                    a, z = cum[:, side, :], cum[:, 1 - side, :]
                    nc.vector.tensor_copy(z[:, 0:reach], a[:, 0:reach])
                    step(nc.vector.tensor_tensor(z[:, reach:NE], a[:, reach:NE], a[:, 0:NE - reach], ALU.add))
                    side, reach = 1 - side, 2 * reach
                wide = [1, NT, NE - 1]
                step(nc.vector.tensor_tensor(
                    before[:, 0, :, :], cum[one, side, 0:NE - 1].rearrange("p (a e) -> p a e", a=1).broadcast_to(wide),
                    iota_t[:, :].rearrange("p (t a) -> p t a", a=1).broadcast_to(wide), ALU.is_le))
                step(nc.vector.tensor_tensor(
                    before[:, 1, :, :], before[:, 0, :, :],
                    ntile[one, 0:NE - 1].rearrange("p (a e) -> p a e", a=1).broadcast_to(wide), ALU.mult))
                step(nc.vector.reduce_sum(tile_f[:, 0:2, :], before[:, :, :, :], AX_X))
                nc.vector.tensor_copy(tile_e[:, :], tile_f[:, 0, :])
                step(nc.vector.tensor_tensor(tile_f[:, 2, :], iota_t[:, :], tile_f[:, 1, :], ALU.subtract))
                step(nc.vector.tensor_scalar(tile_f[:, 2, :], tile_f[:, 2, :], float(P), None, ALU.mult))
                nc.vector.scalar_tensor_tensor(out=tile_s[:, :], in0=tile_f[:, 0, :], scalar=float(REGION),
                                               in1=tile_f[:, 2, :], op0=ALU.mult, op1=ALU.add).then_inc(s_tiles, 1)

            nc.vector.memset(PV[:, :], 0.0).then_inc(s_pz, 1)
            dve.wait_ge(s_x0, 16)
            stats(0, TT, s_stats)
            dve.wait_ge(s_qkbias, 16 * 2)
            step(nc.vector.tensor_scalar(bq_s[:, :, :], bq_s[:, :, :], WSCALE, None, ALU.mult))
            low_weights(slice(1, 2), 1)
            def pad_queries(r):
                nc.vector.memset(QS[64 * r + 32:64 * r + 64, :, :], 0.0).then_inc(s_qpad, 1)

            pad_queries(0)
            inverse_deviation(0, TT, s_sqrt, 1)
            normalise(0, s_xn)
            low_weights(slice(0, 1), 2)

            def empty_entries():
                dve.wait_ge(s_slotno, 1)
                nc.vector.tensor_scalar(empty[:, :, 0], slot_no, P - 1, TOKENS, ALU.bitwise_and,
                                        ALU.bitwise_or).then_inc(s_empty, 1)

            def other_preparations():
                dve.wait_ge(s_tanh, 1)
                step(nc.vector.tensor_scalar(tg16[:, :], tg[:, :], 1.0 / WSCALE, None, ALU.mult))
                nc.vector.tensor_scalar(bo_b[:, :], bo_b[:, :], tg[:, 0:1], None, ALU.mult).then_inc(s_bias, 1)
                dve.wait_ge(s_gate, 16)
                step(nc.vector.tensor_scalar(gh[:, :, :], g32[:, :, :], WSCALE, None, ALU.mult))
                nc.vector.scalar_tensor_tensor(out=gl[:, :, :].rearrange("p k n -> p (k n)"),
                                               in0=g32[:, :, :].rearrange("p k n -> p (k n)"), scalar=WSCALE,
                                               in1=gh[:, :, :].rearrange("p k n -> p (k n)"),
                                               op0=ALU.mult, op1=ALU.subtract).then_inc(s_gsplit, 1)
                dve.wait_ge(s_const, 1)

            for n, u in enumerate(order):
                kind, b = u[0], u[1]
                if n and order[n - 1] == ("mt", 0, 0):
                    other_preparations()
                    inverse_deviation(TT, TILES, s_sqrt, 2)
                if kind == "xt" and u[2] == 0 and b:
                    normalise(b, s_xn)
                if u == ("k", 0, 1):
                    pad_queries(1)
                if u == ("q", 0, 1):
                    empty_entries()
                if u == ("q", 0, 0):
                    low_weights(slice(2, 4), 3)
                if u == ("v", 0, 0):
                    dve.wait_ge(s_x, 16)
                early_stats = [("v", 0, 0), ("v", 0, 1), ("max", 0, 0, 0, 0)]
                if u in early_stats:
                    t = TT * (early_stats.index(u) + 1)
                    stats(t, t + TT, s_stats)
                if b == B - 1 and (kind, u[-1]) in (("at", 0), ("wo", 0), ("xt2", 0)):
                    last_low(("at", "wo", "xt2").index(kind))
                if kind == "xt2" and u[2] == 0:
                    inverse_deviation(TT * b, TT * (b + 1), s_sqrt2, b + 1)
                    normalise(b, s_xn2)
                dve.wait_ge(s_fill, n + 1)
                src = bank(n)
                if kind in ("xt", "at", "xt2") and n:
                    dve.wait_ge(s_free, n)
                if kind == "xt":
                    last = split(xth[:, u[2], :], xtl[:, u[2], :], src)
                elif kind in "qk":
                    t, c = "qk".index(kind), u[2]
                    if b and t == 1 and c == 0:
                        for g in range(NG):
                            dve.wait_ge(s_stack[g], 16 * 12 * b)
                    high, low = nat[:, t, 0, c, :], nat[:, t, 1, c, :]
                    step(nc.vector.tensor_scalar(high, src, bq_s[:, t, c:c + 1], None, ALU.add))
                    last = nc.vector.scalar_tensor_tensor(out=low, in0=src, scalar=bq_s[:, t, c:c + 1], in1=high,
                                                          op0=ALU.add, op1=ALU.subtract)
                elif kind == "v":
                    if b == 0:
                        dve.wait_ge(s_vone, 1)
                        dve.wait_ge(s_small, 16 * 4)
                    if b >= 2 and u[2] == 0:
                        dve.wait_ge(s_pv, SLOTS * (b - 1))
                    for tt in range(2):
                        last = nc.vector.scalar_tensor_tensor(
                            out=V[:, b % 2, 2 * u[2] + tt, :, 0:DH],
                            in0=src[:, D * tt:D * (tt + 1)].rearrange("p (h d) -> p h d", h=H), scalar=1.0 / WSCALE,
                            in1=bv_b[:, :].rearrange("p (h d) -> p h d", h=H), op0=ALU.mult, op1=ALU.add)
                elif kind == "max":
                    _, _, g, tt, j = u
                    last = nc.vector.reduce_max(mx[:, g % 2, tt, (j % 2) * 2 + j // 2:(j % 2) * 2 + j // 2 + 1],
                                                src, AX_X)
                elif kind == "mt":
                    g = u[2]
                    if b:
                        dve.wait_ge(s_mrow[g], 32 * b)
                    if b:
                        last = nc.vector.scalar_tensor_tensor(out=mrow[:, g, :], in0=WB[0:G, n % NB, :],
                                                              scalar=1.0 / MSCALE, in1=mrow[:, g, :],
                                                              op0=ALU.mult, op1=ALU.add)
                    else:
                        last = nc.vector.tensor_scalar(mrow[:, g, :], WB[0:G, n % NB, :], 1.0 / MSCALE, None, ALU.mult)
                elif kind == "ot":
                    g = u[2]
                    o = src.rearrange("p (t j w) -> p t j w", t=TT, j=G)
                    if b and g == 0:
                        dve.wait_ge(s_fill, number["at", b - 1, 1] + 1)
                    if b or g:
                        emptied(dve, "ot", b - (g == 0), (g - 1) % NG)
                    step(nc.vector.reciprocal(rec[:, :, :], o[:, :, :, DH]))
                    last = nc.vector.tensor_tensor(
                        att[:, :, G * DH * g:G * DH * (g + 1)].rearrange("p t (j d) -> p t j d", j=G),
                        o[:, :, :, 0:DH],
                        rec[:, :, :].rearrange("p t (j a) -> p t j a", a=1).broadcast_to([P, TT, G, DH]), ALU.mult)
                elif kind == "at":
                    last = split(ath[:, u[2], :], atl[:, u[2], :], src)
                elif kind == "wo":
                    if u[2] == 0:
                        dve.wait_ge(s_xbo, b + 1)
                    rows = X[:, TT * b + 2 * u[2]:TT * b + 2 * u[2] + 2, :].rearrange("p t d -> p (t d)")
                    last = nc.vector.scalar_tensor_tensor(out=rows, in0=src, scalar=tg16[:, 0:1], in1=rows,
                                                          op0=ALU.mult, op1=ALU.add)
                elif kind == "xt2":
                    last = split(ath[:, u[2], :], atl[:, u[2], :], src)
                elif kind == "gate":
                    last = choose(b, src, n)
                elif kind == "rank":
                    weigh_choices(b)
                    last = number_slots(b, src)
                last.then_inc(s_free, 1)
                if kind == "wo" and u[2] == 1:
                    dve.wait_ge(s_free, n + 1)
                    stats(TT * b, TT * (b + 1), s_stats2)
            list_tiles()

            def tile_split(i, par):
                dve.wait_ge(s_tx, i + 1)
                if since(i, 2):
                    dve.wait_ge(s_h, i - 1)
                nc.vector.tensor_copy(xs[:, par, 0, :], TX[:, 0:D]).then_inc(s_xhigh, 1)
                dve.wait_ge(s_xhigh, i + 1)
                nc.vector.tensor_tensor(xs[:, par, 1, :], TX[:, 0:D], xs[:, par, 0, :], ALU.subtract).then_inc(s_xs, 1)

            def middle(i, par):
                dve.wait_ge(s_silu, i + 1)
                if since(i, 2):
                    dve.wait_ge(s_tm, i - 1)
                nc.vector.tensor_tensor(mid[:, par, :], HB[:, par, 1, :], silu[:, par, :], ALU.mult).then_inc(s_mid, 1)

            def middle_split(i, par):
                dve.wait_ge(s_tm, i + 1)
                if since(i, 2):
                    dve.wait_ge(s_y, i - 1)
                nc.vector.tensor_copy(ms[:, par, 0, :], TM).then_inc(s_mhigh, 1)
                dve.wait_ge(s_mhigh, i + 1)
                nc.vector.tensor_tensor(ms[:, par, 1, :], TM, ms[:, par, 0, :], ALU.subtract).then_inc(s_ms, 1)

            def expert_step(i, par):
                if not (isinstance(i, int) and i >= NT - 1):
                    tile_split(i + 1, 1 - par)
                if since(i, 1):
                    middle_split(i - 1, 1 - par)
                if not (isinstance(i, int) and i >= NT):
                    middle(i, par)

            tile_split(0, 0)
            for i in range(4):
                expert_step(i, i % 2)
            with dve.Fori(4, NT - 1, 2) as i:
                for o in range(2):
                    expert_step(i + o, o)
            for i in range(NT - 1, NT + 1):
                expert_step(i, i % 2)
        @block.tensor
        def _(pe):
            count = [0]

            def three(dst, sh, sl, mh, ml, first, last):
                nc.tensor.matmul(dst, sh, mh, start=first, stop=False)
                nc.tensor.matmul(dst, sh, ml, start=False, stop=False)
                return nc.tensor.matmul(dst, sl, mh, start=False, stop=last)

            def unit(u):
                n = count[0]
                count[0] += 1
                assert order[n] == u
                kind, b = u[0], u[1]
                if n >= NB:
                    pe.wait_ge(s_free, n - NB + 1)
                dst = WB[:, n % NB, :]
                if kind == "xt":
                    pe.wait_ge(s_xn, b + 1)
                    for t in range(TT):
                        last = nc.tensor.transpose(dst[:, P * t:P * (t + 1)], xn[:, t, P * u[2]:P * (u[2] + 1)], ident[:, :])
                elif kind in "qk":
                    t, c = "qk".index(kind), u[2]
                    if kind == "q":
                        emptied(pe, "xt", b, 1)
                    else:
                        pe.wait_ge(s_ctsplit, b + 1)
                    if b == 0:
                        pe.wait_ge(s_wl, 2 - t)
                    mh, ml = ((xth, xtl), (cth, ctl))[t]
                    for k in range(KD):
                        last = three(dst, wh[:, t, k, P * c:P * (c + 1)], wl[:, t, k, P * c:P * (c + 1)],
                                     mh[:, k, :], ml[:, k, :], k == 0, k == KD - 1)
                elif kind == "v":
                    if b == 0:
                        pe.wait_ge(s_wl, 3)
                    for tt in range(2):
                        tok = slice(P * (2 * u[2] + tt), P * (2 * u[2] + tt + 1))
                        for k in range(KD):
                            last = three(dst[:, D * tt:D * (tt + 1)], cth[:, k, tok], ctl[:, k, tok],
                                         wh[:, 2, k, :], wl[:, 2, k, :], k == 0, k == KD - 1)
                elif kind == "max":
                    _, _, g, tt, j = u
                    if (tt, j) == (0, 0):
                        pe.wait_ge(s_stack[g], 16 * 12 * (b + 1))
                    r, pair = j % 2, 2 * g + j // 2
                    last = nc.tensor.matmul(dst, QS[:, pair, P * tt:P * (tt + 1)],
                                            KS[:, pair, r, :], start=True, stop=True)
                elif kind == "mt":
                    g = u[2]
                    emptied(pe, "max", b, g, TT - 1, G - 1)
                    for t in range(TT):
                        last = nc.tensor.transpose(dst[0:G, P * t:P * (t + 1)], mx[:, g % 2, t, :], ident[:, :])
                elif kind == "ot":
                    q = NG * b + u[2]
                    pe.wait_ge(s_ot, q + 1)
                    for t in range(TT):
                        last = nc.tensor.transpose(dst[:, P * t:P * (t + 1)], OT[:, q % 2, P * t:P * (t + 1)], ident[:, :])
                elif kind == "at":
                    emptied(pe, "ot", b, NG - 1)
                    for t in range(TT):
                        last = nc.tensor.transpose(dst[:, P * t:P * (t + 1)], att[:, t, P * u[2]:P * (u[2] + 1)], ident[:, :])
                elif kind == "wo":
                    emptied(pe, "at", b, 1)
                    for tt in range(2):
                        tok = slice(P * (2 * u[2] + tt), P * (2 * u[2] + tt + 1))
                        for k in range(KD):
                            last = three(dst[:, D * tt:D * (tt + 1)], ath[:, k, tok], atl[:, k, tok],
                                         wh[:, 3, k, :], wl[:, 3, k, :], k == 0, k == KD - 1)
                elif kind == "xt2":
                    pe.wait_ge(s_xn2, b + 1)
                    for t in range(TT):
                        last = nc.tensor.transpose(dst[:, P * t:P * (t + 1)], xn[:, t, P * u[2]:P * (u[2] + 1)], ident[:, :])
                elif kind == "gate":
                    emptied(pe, "xt2", b, 1)
                    if b == 0:
                        pe.wait_ge(s_gsplit, 1)
                    for t in range(TT):
                        for k in range(KD):
                            last = three(dst[:, NE * t:NE * (t + 1)], ath[:, k, P * t:P * (t + 1)],
                                         atl[:, k, P * t:P * (t + 1)], gh[:, k, :], gl[:, k, :], k == 0, k == KD - 1)
                elif kind == "rank":
                    emptied(pe, "gate", b)
                    if b == 0:
                        pe.wait_ge(s_const, 1)
                    for t in range(TT + 1):
                        for a in range(min(t + 1, TT)):
                            last = nc.tensor.matmul(dst[:, NE * t:NE * (t + 1)], (earlier if a == t else ones)[:, :],
                                                    both[:, a, :], start=(a == 0), stop=(a == min(t, TT - 1)))
                last.then_inc(s_fill, 1)

            def scores(n):
                s, pp = divmod(n, 2)
                b, s = divmod(s, SLOTS)
                g, st = divmod(s, TT)
                if (st, pp) == (0, 0):
                    pe.wait_ge(s_mrow[g], 32 * (b + 1))
                if n >= 2:
                    pe.wait_ge(s_exp, n - 1)
                for r in range(2):
                    last = nc.tensor.matmul(SC[:, n % 2, r, :], KS[:, 2 * g + pp, r, P * st:P * (st + 1)],
                                            QS[:, 2 * g + pp, :], start=True, stop=True)
                last.then_inc(s_score, 1)

            def weigh(s):
                b, q = divmod(s, SLOTS)
                g, st = divmod(q, TT)
                pe.wait_ge(s_exp, 2 * s + 2)
                if st == 0 and s:
                    pe.wait_ge(s_ot, s // TT)
                if st == 0 and g == 0:
                    emptied(pe, "v", b, 1)
                for j in range(G):
                    last = nc.tensor.matmul(PV[32 * j:32 * j + VW, :], V[:, b % 2, st, G * g + j, :],
                                            E[:, (2 * s + j // 2) % 4, j % 2, :], start=(st == 0), stop=(st == TT - 1))
                last.then_inc(s_pv, 1)

            pe.wait_ge(s_ident, 1)
            pe.wait_ge(s_pz, 1)
            for u in slot_units[-1]:
                unit(u)
            scores(0)
            scores(1)
            for s in range(B * SLOTS):
                units = slot_units[s]
                for u in units[:len(units) // 2]:
                    unit(u)
                if s + 1 < B * SLOTS:
                    scores(2 * s + 2)
                for u in units[len(units) // 2:]:
                    unit(u)
                if s + 1 < B * SLOTS:
                    scores(2 * s + 3)
                weigh(s)
            for s in range(B * SLOTS, B * SLOTS + 12):
                for u in slot_units[s]:
                    unit(u)

            def turn_tile(i, par):
                pe.wait_ge(s_xg[par], i * 8 - 8 * par + 16)
                if since(i, 1):
                    pe.wait_ge(s_xs, i)
                for k in range(KD):
                    last = nc.tensor.transpose(TX[:, P * k:P * (k + 1)], xg[:, par, P * k:P * (k + 1)], ident[:, :])
                last.then_inc(s_tx, 1)

            def hidden(i, par, e):
                pe.wait_ge(s_xs, i + 1)
                if since(i, 2):
                    pe.wait_ge(s_mid, i - 1)
                for k in range(KD):
                    xh, xl = (xs[:, par, h, P * k:P * (k + 1)] for h in range(2))
                    for m in range(2):
                        high, low = (WE[:, bass.ds(e, 1), 2 * m + h, HID * k:HID * (k + 1)].rearrange(
                            "p a n -> p (a n)") for h in range(2))
                        last = three(HB[:, par, m, :], xh, xl, high, low, k == 0, k == KD - 1)
                last.then_inc(s_h, 1)

            def turn_middle(i, par):
                pe.wait_ge(s_mid, i + 1)
                if since(i, 1):
                    pe.wait_ge(s_ms, i)
                for k in range(KH):
                    last = nc.tensor.transpose(TM[:, P * k:P * (k + 1)], mid[:, par, P * k:P * (k + 1)], ident[:, :])
                last.then_inc(s_tm, 1)

            def output(i, par, e):
                pe.wait_ge(s_ms, i + 1)
                if since(i, 2):
                    pe.wait_ge(s_ysb, i - 1)
                for k in range(KH):
                    mh, ml = (ms[:, par, h, P * k:P * (k + 1)] for h in range(2))
                    high, low = (WE[:, bass.ds(e, 1), 4 + h, D * k:D * (k + 1)].rearrange(
                        "p a n -> p (a n)") for h in range(2))
                    last = three(YB[par][:, 0:D], mh, ml, high, low, k == 0, k == KH - 1)
                last.then_inc(s_y, 1)

            def expert(i):
                return pe.value_load(tile_e[0:1, bass.ds(i, 1)], min_val=0, max_val=NE - 1)

            pe.wait_ge(s_tiles, 1)
            pe.wait_ge(s_wsplit, 3 * (NE - 1))
            pe.wait_ge(s_last_low, 3)
            def expert_step(i, par):
                if not (isinstance(i, int) and i >= NT):
                    hidden(i, par, expert(i))
                if not (isinstance(i, int) and i >= NT - 1):
                    turn_tile(i + 1, 1 - par)
                if since(i, 1) and not (isinstance(i, int) and i > NT):
                    turn_middle(i - 1, 1 - par)
                if since(i, 2):
                    output(i - 2, par, expert(i - 2))

            turn_tile(0, 0)
            for i in range(4):
                expert_step(i, i % 2)
            with pe.Fori(4, NT - 1, 2) as i:
                for o in range(2):
                    expert_step(i + o, o)
            for i in range(NT - 1, NT + 2):
                expert_step(i, i % 2)


_NAMES = ["x", "ctxT", "g_xattn", "g_ffn", "wq", "bq", "wk", "bk", "wv", "bv", "woT", "bo", "gate", "w0", "w1", "wo"]


def kernel(x, ctx_1024, g_xattn, g_ffn, L0_xattn_Wq, L0_xattn_bq, L0_xattn_Wk, L0_xattn_bk, L0_xattn_Wv, L0_xattn_bv,
           L0_xattn_Wo, L0_xattn_bo, L0_ffn_gate_kernel, L0_ffn_w0_kernel, L0_ffn_w1_kernel, L0_ffn_wo_kernel):
    import numpy as np
    import concourse.bacc as bacc
    from concourse import mybir as mb
    from concourse.bass_utils import run_bass_kernel_spmd

    def packed(a):
        return np.ascontiguousarray(np.asarray(a))

    B, S, D = x.shape
    H, _, DH = L0_xattn_Wq.shape
    heads = [2 * (2 * (i // 2) + c) + i % 2 for c in range(2) for i in range(H // 2)]

    def columns(w, order):
        return packed(np.asarray(w)[order].transpose(1, 0, 2).reshape(D, H * DH))

    arrays = {
        "x": packed(x).reshape(B * S, D),
        "ctxT": packed(np.asarray(ctx_1024).transpose(0, 2, 1)),
        "g_xattn": packed(g_xattn), "g_ffn": packed(g_ffn),
        "wq": columns(L0_xattn_Wq, heads), "bq": packed(np.asarray(L0_xattn_bq)[heads].reshape(2, -1).T),
        "wk": columns(L0_xattn_Wk, heads), "bk": packed(np.asarray(L0_xattn_bk)[heads].reshape(2, -1).T),
        "wv": columns(L0_xattn_Wv, list(range(H))), "bv": packed(np.asarray(L0_xattn_bv).reshape(-1)),
        "woT": packed(np.asarray(L0_xattn_Wo).T), "bo": packed(L0_xattn_bo),
        "gate": packed(L0_ffn_gate_kernel),
        "w0": packed(L0_ffn_w0_kernel), "w1": packed(L0_ffn_w1_kernel), "wo": packed(L0_ffn_wo_kernel),
    }
    arrays["g_xattn"] = arrays["g_xattn"].reshape(-1)
    arrays["g_ffn"] = arrays["g_ffn"].reshape(-1)
    nc = bacc.Bacc("TRN2", target_bir_lowering=False, num_devices=1)
    aps = [nc.dram_tensor(f"in_{n}", arrays[n].shape, mb.dt.from_np(arrays[n].dtype), kind="ExternalInput").ap()
           for n in _NAMES]
    out = nc.dram_tensor("out", (B * S + P, D), mb.dt.float32, kind="ExternalOutput").ap()
    program(nc, *aps, out)
    r = run_bass_kernel_spmd(nc, [{f"in_{n}": arrays[n] for n in _NAMES}], core_ids=[0])
    return r.results[0]["out"][:B * S].reshape(B, S, D)
```

```python
import concourse.bass as bass
from concourse import mybir
from contextlib import ExitStack

F32 = mybir.dt.float32
F16 = mybir.dt.float16
I32 = mybir.dt.int32
U32 = mybir.dt.uint32
ALU = mybir.AluOpType
ACT = mybir.ActivationFunctionType
AX_X = mybir.AxisListType.X

P = 128
EPS = 1e-5
WSCALE = 16.0
PACE = 3
MSCALE = 256.0


def program(nc, x, ctxT, g_xattn, g_ffn, wq, bq, wk, bk, wv, bv, woT, bo, gate, w0, w1, wo, out):
    TOKENS, D = x.shape
    B, _, S = ctxT.shape
    KD = D // P
    TT = S // P
    TILES = TOKENS // P
    H = 16
    DH = D // H
    G = 4
    NG = H // G
    VW = DH + 1
    KS_ROWS = 3 * DH
    SLOTS = NG * TT
    _, NE = gate.shape
    HID = w0.shape[2]
    KH = HID // P
    REGION = TOKENS
    NT = (2 * TOKENS + NE * (P - 1)) // P
    FIRST = 12
    KNOWN = TOKENS - S
    assert FIRST <= (2 * KNOWN - NE * (P - 1)) / P and FIRST % 2 == 0
    SPARE = (NE - 1) * REGION + NT * P
    SCORE_SCALE = 1.0 / (float(DH) ** 0.5 * WSCALE * WSCALE)

    with ExitStack() as ctx:
        def sb(name, shape, dt):
            return ctx.enter_context(nc.sbuf_tensor(name, shape, dt))

        def psum(name, shape, dt=F32):
            return ctx.enter_context(nc.psum_tensor(name, shape, dt))

        def sem(name):
            return ctx.enter_context(nc.semaphore(name))

        ident = sb("ident", [P, P], F32)
        pad = sb("pad", [P, 1], F32)
        WE = sb("WE", [P, NE, 6, KD * HID], F16)
        last_expert = WE[:, NE - 1, :, :].rearrange("p a n -> p (a n)")
        X = sb("X", [P, TILES, D], F32)
        stage = sb("stage", [P, 4, KD, D], F32)
        wh = sb("wh", [P, 4, KD, D], F16)
        wl = sb("wl", [P, 4, KD, D], F16)
        bq_s = sb("bq_s", [P, 2, 2], F32)
        bv_b = sb("bv_b", [P, D], F32)
        bo_b = sb("bo_b", [P, D], F32)
        gains = sb("gains", [P, 2], F32)
        tg = sb("tg", [P, 2], F32)
        tg16 = sb("tg16", [P, 2], F32)
        st6 = sb("st6", [P, TILES, 6], F32)
        mv = sb("mv", [P, TILES, 2], F32)
        sd = sb("sd", [P, TILES], F32)
        nw = sb("nw", [P, 2, TILES], F32)
        rstd = sb("rstd", [P, TILES], F32)
        xn = sb("xn", [P, TT, D], F32)
        xth = sb("xth", [P, KD, S], F16)
        xtl = sb("xtl", [P, KD, S], F16)
        c32 = sb("c32", [P, KD, S], F32)
        cth = last_expert[:, 4096:5120].rearrange("p (k s) -> p k s", k=KD)
        ctl = last_expert[:, 5120:6144].rearrange("p (k s) -> p k s", k=KD)
        nat = sb("nat", [P, 2, 2, 2, S], F16)
        QS = last_expert[:, 0:4096].rearrange("p (h s) -> p h s", h=H // 2)
        KS = sb("KS", [P, H // 2, 2, S], F16)
        V = sb("V", [P, 2, TT, H, VW], F32)
        mx = sb("mx", [P, 2, TT, G], F32)
        small = sb("small", [P, NG * S], F16)
        mrow = small[0:G, :].rearrange("j (g s) -> j g s", g=NG)
        E = sb("E", [P, 4, 2, S], F32)
        OT = sb("OT", [P, 2, S], F32)
        rec = sb("rec", [P, TT, G], F32)
        att = sb("att", [P, TT, D], F32)
        ath, atl = xth, xtl

        g32 = sb("g32", [P, KD, NE], F32)
        gh = sb("gh", [P, KD, NE], F16)
        gl = sb("gl", [P, KD, NE], F16)
        earlier = sb("earlier", [P, P], F16)
        ones = sb("ones", [P, P], F16)
        iota_e = sb("iota_e", [P, NE], F32)
        entry = sb("entry", [P, TILES, 2, 2], I32)
        weight = entry[:, :, :, 1].bitcast(F32)
        lg = sb("lg", [P, TT, NE], F32)
        m8 = sb("m8", [P, TT, 8], F32)
        i8 = sb("i8", [P, TT, 8], U32)
        idf = sb("idf", [P, TT, 2], F32)
        pick = sb("pick", [P, 2, TILES, NE], F32)
        both = sb("both", [P, TT, NE], F16)
        gap = sb("gap", [P, TT], F32)
        egap = sb("egap", [P, TT], F32)
        den = sb("den", [P, TT], F32)
        next_slot = sb("next_slot", [P, NE], F32)
        slot_of = sb("slot_of", [P, TT, NE], F32)
        chosen = sb("chosen", [P, TT, NE], F32)
        slot = sb("slot", [P, 2, TILES], I32)
        cnt = sb("cnt", [P, NE], F32)
        cnt_i = sb("cnt_i", [P, 2, NE], I32)
        ntile = sb("ntile", [P, NE], F32)
        cum = sb("cum", [P, 2, NE], F32)
        left = sb("left", [P, NE], F32)
        used = sb("used", [P, NE], F32)
        LIST = 32
        row = small[LIST:LIST + 1, :]
        tile_e = row[:, 0:2 * NT].bitcast(I32)
        tile_s = row[:, 2 * NT:4 * NT].bitcast(I32)
        iota_t = row[:, 4 * NT:6 * NT].bitcast(F32)
        tile_f = row[:, 6 * NT:12 * NT].bitcast(F32).rearrange("p (a t) -> p a t", a=3)
        REST = NT - FIRST
        before = row[:, 12 * NT:12 * NT + 4 * REST * (NE - 1)].bitcast(F32).rearrange("p (a t e) -> p a t e", a=2, t=REST)
        slots_f = sb("slots_f", [P, 2, TILES], F32)
        filled = sb("filled", [P, NT, 2], I32)
        Ef = E[:, :, :, :].rearrange("p a b n -> p (a b n)")
        xg = Ef[:, 0:512].rearrange("p (b d) -> p b d", b=2)
        silu = Ef[:, 512:1536].rearrange("p (b n) -> p b n", b=2)
        mid = Ef[:, 1536:2560].rearrange("p (b n) -> p b n", b=2)
        ysb = Ef[:, 2560:3072].rearrange("p (b n) -> p b n", b=2)
        natf = nat[:, :, :, :, :].rearrange("p a b c n -> p (a b c n)")
        xs = natf[:, 0:1024].rearrange("p (b h n) -> p b h n", b=2, h=2)
        ms = natf[:, 1024:3072].rearrange("p (b h n) -> p b h n", b=2, h=2)
        empty = Ef[:, 0:2 * (SPARE // P)].bitcast(I32).rearrange("p (n a) -> p n a", a=2)
        slot_no = Ef[:, 512:512 + SPARE // P].bitcast(I32)
        nil = Ef[:, 1024:1024 + D]
        rows_d = nc.dram_tensor("rows_by_token", (TOKENS + P, D), F32, kind="Internal").ap()
        slot_d = nc.dram_tensor("entry_by_slot", (SPARE, 2), I32, kind="Internal").ap()

        SC = psum("SC", [P, 2, 2, S])
        PV = psum("PV", [P, S])
        NB = 3
        WB = psum("WB", [P, NB, 512])
        HB = SC
        TX, TM = WB[:, 2, :], WB[:, 1, :]

        def output_bank(i, par):
            return PV if isinstance(i, int) and i < FIRST - 2 or par else WB[:, 0, :]

        s_x0 = sem("x_first_batch_loaded")
        s_x = sem("x_other_batches_loaded")
        s_wk = sem("key_weights_loaded")
        s_wq = sem("query_weights_loaded")
        s_w2 = sem("value_and_output_weights_loaded")
        s_qkbias = sem("query_and_key_biases_loaded")
        s_small = sem("other_biases_and_gains_loaded")
        s_ctx = sem("context_loaded")
        s_ident = sem("identity_made")
        s_vone = sem("value_ones_set")
        s_qpad = sem("query_rows_padded")
        s_pad = sem("zero_made")
        s_kpad = sem("key_rows_padded")
        s_zpad = sem("other_heads_rows_cleared")
        s_wh = sem("weight_high_parts_made")
        s_wl = sem("weight_low_parts_made")
        s_ctsplit = sem("context_split")
        s_bias = sem("biases_scaled")
        s_tanh = sem("gains_tanh_made")
        s_stats = sem("variances_ready")
        s_sqrt = sem("deviations_ready")
        s_xn = sem("rows_normalised")
        s_xbo = sem("output_bias_added")
        s_fill = sem("work_bank_filled")
        s_free = sem("work_bank_emptied")
        s_dve = sem("vector_step_done")
        s_pool = sem("pool_step_done")
        s_stack = [sem(f"group{g}_stacked") for g in range(NG)]
        s_mrow = [sem(f"group{g}_maxima_placed") for g in range(NG)]
        s_score = sem("scores_done")
        s_exp = sem("exponentials_done")
        s_pv = sem("values_weighted")
        s_ot = sem("attention_output_copied")
        s_pz = sem("output_bank_zeroed")
        s_gate = sem("router_weights_loaded")
        s_gsplit = sem("router_weights_split")
        s_slotno = sem("slot_numbers_made")
        s_const = sem("router_constants_made")
        s_zero = sem("token_table_cleared")
        s_rows = sem("rows_stored")
        s_gap = sem("choice_gaps_ready")
        s_egap = sem("choice_gaps_exponentiated")
        s_xhigh = sem("tile_high_part_made")
        s_mhigh = sem("middle_high_part_made")
        s_stats2 = sem("expert_input_variances_ready")
        s_sqrt2 = sem("expert_input_deviations_ready")
        s_xn2 = sem("expert_input_normalised")
        s_share = sem("choices_weighed")
        s_slot = sem("slots_numbered")
        s_idput = sem("tokens_placed")
        s_tiles = sem("tiles_listed")
        s_we = [sem(f"expert_weights_loaded{i}") for i in range(2)]
        s_whigh = sem("expert_weight_high_parts_made")
        s_w16 = sem("expert_weights_scaled")
        s_cth = sem("context_high_parts_made")
        s_empty = sem("empty_entries_made")
        s_wsplit = sem("expert_weights_split")
        NL = 4
        s_ids = [sem(f"tile_entries_loaded{i}") for i in range(NL)]
        s_xg = [sem(f"tile_rows_gathered{i}") for i in range(2)]
        s_tx = sem("tile_turned")
        s_xs = sem("tile_split")
        s_h = sem("hidden_sums_done")
        s_silu = sem("silu_done")
        s_mid = sem("middle_done")
        s_tm = sem("middle_turned")
        s_ms = sem("middle_split")
        s_y = sem("expert_output_done")
        s_ysb = sem("expert_output_copied")
        s_base = sem("attention_result_stored")
        s_add = sem("expert_output_added")

        slot_units = {s: [] for s in range(-1, B * SLOTS + 12)}

        def second_half(b):
            return SLOTS * (b + 1) + (4 if b < B - 2 else 2)

        def max_slots(b, g):
            if b == 0:
                return ((-1, -1), (-1, 1), (2, 5), (5, 8))[g]
            home = SLOTS * b + TT * g - (7 if b == B - 1 else 10)
            return home, home + TT - 1

        def place(s, *unit):
            slot_units[s].append(unit)

        for b in range(B):
            base = SLOTS * (b - 1)
            at = (lambda o: -1) if b == 0 else (lambda o: base + o)
            for k in range(KD):
                place(at(0 + k), "xt", b, k)
            if b == 0:
                for c in range(2):
                    place(-1, "k", b, c)
            for c in range(2):
                if b:
                    place(at(2 + c), "k", b, c)
                place(at(2 + c), "q", b, c)
            for h in range(2):
                place(at(4 + h), "v", b, h)
        for b in range(B):
            for g in range(NG):
                first, last = max_slots(b, g)
                for n in range(TT * G):
                    place(first + (last - first + 1) * n // (TT * G), "max", b, g, n // G, n % G)
                place(last, "mt", b, g)
                place(SLOTS * b + TT * (g + 1) + 1, "ot", b, g)
        for b in range(B):
            end = second_half(b)
            for c in range(2):
                place(end, "at", b, c)
            for h in range(2):
                place(end + 1, "wo", b, h)
            for k in range(KD):
                place(end + 3, "xt2", b, k)
            place(end + 4, "gate", b)
            place(end + 6, "rank", b)
        order = [u for s in sorted(slot_units) for u in slot_units[s]]
        number = {u: n for n, u in enumerate(order)}
        LISTED = 5
        LATE = len([u for q in slot_units if q < B * SLOTS for u in slot_units[q]])
        after_tile = {-1: order[LATE:LATE + 3], 0: order[LATE + 3:LATE + 5], 2: order[LATE + 5:LATE + 7],
                      3: order[LATE + 7:LATE + 8], 4: order[LATE + 8:]}

        def emptied(eng, *unit):
            eng.wait_ge(s_free, number[unit] + 1)

        def part_of(n):
            e, m = divmod(n, 3)
            return e, (0, 2, 1)[m] if e == NE - 1 else m

        LAST_HIGH = (SLOTS * (B - 1) + 6, SLOTS * (B - 1) + 9, SLOTS * (B - 1) + 12)
        LAST_LOW = (SLOTS * (B - 1) + 8, SLOTS * (B - 1) + 10, SLOTS * B)

        def high_slot(n):
            return LAST_HIGH[n - 3 * NE + 3] if n >= 3 * (NE - 1) else 1 + PACE * n // 2

        def low_slot(n):
            return LAST_LOW[n - 3 * NE + 3] if n >= 3 * (NE - 1) else high_slot(n)

        def context_slot(b):
            return SLOTS * (b - 2) + 7

        def since(i, first):
            return not isinstance(i, int) or i >= first

        def part_stage(n):
            return stage[:, 2 * (n % 2):2 * (n % 2) + 2, :, :].rearrange("p a k n -> p (a k n)")

        block = ctx.enter_context(nc.Block())

        @block.sync
        def _(sp):
            xr = x.rearrange("(t p) d -> p t d", p=P)
            sp.dma_start(stage[:, 1, :, :], wk.rearrange("(k p) n -> p k n", p=P)).then_inc(s_wk, 16)
            sp.dma_start(X[:, 0:TT, :], xr[:, 0:TT, :]).then_inc(s_x0, 16)
            sp.dma_start(stage[:, 0, :, :], wq.rearrange("(k p) n -> p k n", p=P)).then_inc(s_wq, 16)
            for n, v in enumerate((bq, bk)):
                sp.dma_start(bq_s[:, n, :], v).then_inc(s_qkbias, 16)
            for n, w in ((2, wv), (3, woT)):
                sp.dma_start(stage[:, n, :, :], w.rearrange("(k p) n -> p k n", p=P)).then_inc(s_w2, 16)
            sp.dma_start(X[:, TT:TILES, :], xr[:, TT:TILES, :]).then_inc(s_x, 16)
            for t, v in ((bv_b, bv), (bo_b, bo)):
                sp.dma_start(t[:, :], v.rearrange("(a n) -> a n", a=1).broadcast_to([P, D])).then_inc(s_small, 16)
            sp.dma_start(g32[:, :, :], gate.rearrange("(k p) n -> p k n", p=P)).then_inc(s_gate, 16)
            for n, v in enumerate((g_xattn, g_ffn)):
                sp.dma_start(gains[:, n:n + 1], v.rearrange("(a n) -> a n", a=1).broadcast_to([P, 1])).then_inc(s_small, 16)

            def stack(t, b, g):
                if b:
                    sp.wait_ge(s_score, 2 * (SLOTS * (b - 1) + TT * (g + 1)))
                elif g == 0:
                    sp.wait_ge(*(s_qpad, 2) if t == 0 else (s_kpad, 2))
                    sp.wait_ge(s_zpad, 2)
                if g == 0:
                    emptied(sp, "qk"[t], b, 1)
                for r in range(2):
                    i = 2 * g + r
                    for o, part in enumerate(((0, 0, 1), (0, 1, 0))[t]):
                        rows = slice(64 * r + DH * o, 64 * r + DH * (o + 1))
                        to = QS[rows, 2 * g:2 * g + 2, :] if t == 0 else KS[rows, 2 * g:2 * g + 2, r, :]
                        sp.dma_start(to, nat[DH * i:DH * i + DH, t, part, :, :]).then_inc(s_stack[g], 16)

            def stack_keys(b, g):
                stack(1, b, g)

            def stack_queries(b, g):
                stack(0, b, g)

            def maxima(b, g):
                emptied(sp, "mt", b, g)
                for r in range(2):
                    row = 64 * r + KS_ROWS
                    sp.dma_start(QS[row:row + 1, 2 * g:2 * g + 2, :],
                                 mrow[2 * r:2 * r + 2, g, :]).then_inc(s_mrow[g], 16)

            def store_rows(b, g):
                sp.wait_ge(s_xn2, b + 1)
                sp.dma_start(rows_d[0:TOKENS, :].rearrange("(t p) d -> p t d", p=P)[:, TT * b:TT * (b + 1), :],
                             xn[:, :, :]).then_inc(s_rows, 16)

            def clear(b, g):
                sp.wait_ge(s_empty, 1)
                sp.wait_ge(s_const, 1)
                sp.dma_start(slot_d.rearrange("(p n) a -> p n a", p=P), empty).then_inc(s_zero, 16)
                sp.dma_start(rows_d[TOKENS:TOKENS + P, :], nil).then_inc(s_zero, 16)
                sp.dma_start(out[TOKENS:TOKENS + P, :], nil).then_inc(s_zero, 16)

            def store_base(b, g):
                emptied(sp, "wo", b, 1)
                sp.dma_start(out[0:TOKENS, :].rearrange("(t p) d -> p t d", p=P)[:, TT * b:TT * (b + 1), :],
                             X[:, TT * b:TT * (b + 1), :]).then_inc(s_base, 16)

            def load_entries(i, lane):
                at = sp.value_load(tile_s[0:1, bass.ds(i, 1)], min_val=0, max_val=SPARE - P)
                if since(i, NL):
                    sp.wait_ge(s_ids[lane], (i - lane) * (16 // NL))
                sp.dma_start(filled[:, bass.ds(i, 1), :], slot_d[bass.ds(at, P), :].rearrange(
                    "p (a c) -> p a c", a=1)).then_inc(s_ids[lane], 16)

            def first_entries(b, g):
                sp.wait_ge(s_idput, 16 * 2 * TT * (B - 1))
                sp.wait_ge(s_tiles, 1)
                for i in range(FIRST):
                    load_entries(i, i % NL)

            jobs = [(-4.5, 3, clear, 0, 0)]
            for b in range(B):
                jobs.append((second_half(b) + 3, 2, store_rows, b, 0))
                jobs.append((second_half(b) + 2, 3, store_base, b, 0))
                if b == B - 1:
                    jobs.append((B * SLOTS - 1, 4, first_entries, b, 0))
                for g in range(NG):
                    when = SLOTS * b + TT * (g - 3) if b else g - NG - 2
                    jobs.append((when, 0, stack_keys, b, g))
                    jobs.append((when, 0.5, stack_queries, b, g))
                    jobs.append((max_slots(b, g)[1] if b or g else -3.5, 1, maxima, b, g))
            for _, _, job, b, g in sorted(jobs, key=lambda j: (j[0], j[1], j[3], j[4])):
                job(b, g)

            sp.wait_ge(s_idput, 16 * 2 * TILES)
            sp.wait_ge(s_tiles, 2)
            whole = NT // NL * NL
            with sp.Fori(FIRST, whole, NL) as i:
                for lane in range(NL):
                    load_entries(i + lane, lane)
            for i in range(whole, NT):
                load_entries(i, i % NL)
            sp.wait_ge(s_base, 16 * B)
            sp.wait_ge(s_add, 16 * NT)

        @block.gpsimd
        def _(pool):
            steps = [0]

            def step(ins):
                steps[0] += 1
                ins.then_inc(s_pool, 1)
                pool.wait_ge(s_pool, steps[0])

            pool.dma_start(c32[:, :, :], ctxT[0].rearrange("(k p) s -> p k s", p=P)).then_inc(s_ctx, 16)
            nc.gpsimd.memset(pad[:, :], 0.0).then_inc(s_pad, 1)
            step(nc.gpsimd.memset(ident[:, :], 0.0))
            nc.gpsimd.affine_select(out=ident[:, :], in_=ident[:, :], compare_op=ALU.not_equal, fill=1.0,
                                    base=0, pattern=[[-1, P]], channel_multiplier=1).then_inc(s_ident, 1)
            pool.wait_ge(s_ident, 1)

            def pad_keys(r):
                nc.gpsimd.memset(KS[64 * r + 32:64 * r + 64, :, r, :], -MSCALE).then_inc(s_kpad, 1)
                pool.wait_ge(s_kpad, r + 1)

            def constants():
                step(nc.gpsimd.memset(ones[:, :], 1.0))
                step(nc.gpsimd.memset(earlier[:, :], 1.0))
                step(nc.gpsimd.affine_select(out=earlier[:, :], in_=earlier[:, :], compare_op=ALU.is_gt, fill=0.0,
                                             base=0, pattern=[[1, P]], channel_multiplier=-1))
                step(nc.gpsimd.iota(iota_e[:, :], pattern=[[1, NE]], base=0, channel_multiplier=0,
                                    allow_small_or_imprecise_dtypes=True))
                step(nc.gpsimd.iota(iota_t[:, :], pattern=[[1, NT]], base=0, channel_multiplier=0,
                                    allow_small_or_imprecise_dtypes=True))
                step(nc.gpsimd.iota(next_slot[:, :], pattern=[[REGION, NE]], base=0, channel_multiplier=0,
                                    allow_small_or_imprecise_dtypes=True))
                nc.gpsimd.iota(entry[:, :, :, 0], pattern=[[P, TILES], [0, 2]], base=0,
                               channel_multiplier=1).then_inc(s_const, 1)

            def load_part(n):
                e, m = part_of(n)
                src = (w0, w1, wo)[m][e]
                pool.dma_start(part_stage(n).rearrange("p (k n) -> p k n", n=src.shape[1]),
                               src.rearrange("(k p) n -> p k n", p=P)).then_inc(
                                   s_we[n % 2], 16)

            def low_part(n):
                e, m = part_of(n)
                if n == 0:
                    pool.wait_ge(s_wl, 3)
                    load_part(0)
                    load_part(1)
                if n in (3 * NE - 3, 3 * NE - 1):
                    pool.wait_ge(s_score, 2 * SLOTS * (B - 1) + (4 if n == 3 * NE - 3 else 8) * TT)
                pool.wait_ge(s_w16, n + 1)
                nc.gpsimd.tensor_tensor(WE[:, e, 2 * m + 1, :], part_stage(n), WE[:, e, 2 * m, :],
                                        ALU.subtract).then_inc(s_wsplit, 1)
                pool.wait_ge(s_wsplit, n + 1)
                if n + 2 < 3 * NE:
                    load_part(n + 2)

            def low_context(b):
                pool.wait_ge(s_cth, b + 1)
                nc.gpsimd.tensor_tensor(ctl[:, :, :], c32[:, :, :], cth[:, :, :], ALU.subtract).then_inc(s_ctsplit, 1)
                if b + 1 < B:
                    pool.wait_ge(s_ctsplit, b + 1)
                    pool.dma_start(c32[:, :, :], ctxT[b + 1].rearrange("(k p) s -> p k s", p=P)).then_inc(s_ctx, 16)

            def output_bias(b):
                pool.wait_ge(s_xn, b + 1)
                if b == 0:
                    pool.wait_ge(s_bias, 1)
                rows = X[:, TT * b:TT * (b + 1), :]
                nc.gpsimd.tensor_tensor(rows, rows, bo_b[:, :].rearrange("p (a d) -> p a d", a=1).broadcast_to([P, TT, D]),
                                        ALU.add).then_inc(s_xbo, 1)

            def place_entries(b):
                pool.wait_ge(s_slot, b + 1)
                if b == 0:
                    pool.wait_ge(s_zero, 16 * 3)
                for t in range(TT * b, TT * (b + 1)):
                    for k in range(2):
                        pool.indirect_dma_start(slot_d[:, :], bass.IndirectOffsetOnAxis(slot[:, k, t:t + 1].bitcast(U32), 0),
                                                entry[:, t, k, :], None).then_inc(s_idput, 16)

            pad_keys(0)
            low_context(0)
            pad_keys(1)
            nc.gpsimd.memset(V[:, :, :, :, :], 1.0).then_inc(s_vone, 1)
            pool.wait_ge(s_vone, 1)
            step(nc.gpsimd.memset(nil, 0.0))
            step(nc.gpsimd.memset(empty, 0))
            nc.gpsimd.iota(slot_no, pattern=[[1, SPARE // P]], base=0, channel_multiplier=SPARE // P).then_inc(s_slotno, 1)
            constants()
            jobs = [(low_slot(n), 0, low_part, n) for n in range(3 * NE)]
            for b in range(B):
                if b:
                    jobs.append((context_slot(b), 1, low_context, b))
                jobs.append((SLOTS * (b - 1) + 3, 2, output_bias, b))
                if b < B - 1:
                    jobs.append((second_half(b) + 6.5, 3, place_entries, b))
            for _, _, job, arg in sorted(jobs, key=lambda j: j[0:2]):
                job(arg)

            def gather(i):
                pool.wait_ge(s_ids[i % NL], 16 * (i // NL + 1))
                if i >= 2:
                    pool.wait_ge(s_tx, i - 1)
                pool.indirect_dma_start(xg[:, i % 2, :], None, (rows_d[0:KNOWN, :] if i < FIRST else rows_d[:, :]), bass.IndirectOffsetOnAxis(
                    filled[:, i, 0:1].bitcast(U32), 0)).then_inc(s_xg[i % 2], 16)

            def scatter(i):
                pool.wait_ge(s_ysb, i + 1)
                if i:
                    pool.wait_ge(s_add, 16 * i)
                pool.indirect_dma_start((out[0:KNOWN, :] if i < FIRST else out[:, :]), bass.IndirectOffsetOnAxis(filled[:, i, 0:1].bitcast(U32), 0),
                                        ysb[:, i % 2, :], None, compute_op=ALU.add).then_inc(s_add, 16)

            pool.wait_ge(s_rows, 16 * (B - 1))
            pool.wait_ge(s_base, 16 * (B - 1))
            pool.wait_ge(s_pv, B * SLOTS)
            PLACE = 10
            LAG = 6
            for i in range(NT + LAG):
                if i == PLACE:
                    for lane in range(NL):
                        pool.wait_ge(s_ids[lane], 16 * (FIRST // NL))
                    place_entries(B - 1)
                if i == FIRST:
                    pool.wait_ge(s_rows, 16 * B)
                    pool.wait_ge(s_base, 16 * B)
                if i < NT:
                    gather(i)
                if i >= LAG:
                    scatter(i - LAG)

        @block.scalar
        def _(act):
            def copy_output(act, q):
                act.wait_ge(s_pv, TT * (q + 1))
                if q >= 2:
                    emptied(act, "ot", (q - 2) // NG, (q - 2) % NG)
                nc.scalar.activation(OT[:, q % 2, :], PV[:, :], ACT.Copy).then_inc(s_ot, 1)

            def second_norm(b):
                act.wait_ge(s_stats2, b + 1)
                nc.scalar.activation(sd[:, TT * b:TT * (b + 1)], nw[:, 0, TT * b:TT * (b + 1)], ACT.Sqrt).then_inc(s_sqrt2, 1)

            def choice_exp(b):
                act.wait_ge(s_gap, b + 1)
                nc.scalar.activation(egap[:, :], gap[:, :], ACT.Exp).then_inc(s_egap, 1)

            def high_context(b):
                act.wait_ge(s_ctx, 16 * (b + 1))
                if b:
                    emptied(act, "v", b - 1, 1)
                nc.scalar.activation(cth[:, :, :], c32[:, :, :], ACT.Copy).then_inc(s_cth, 1)

            def high_part(n):
                e, m = part_of(n)
                act.wait_ge(s_we[n % 2], 16 * (n // 2 + 1))
                if n == 3 * NE - 2:
                    emptied(act, "v", B - 1, 1)
                nc.scalar.activation(WE[:, e, 2 * m, :], part_stage(n), ACT.Copy, scale=WSCALE).then_inc(s_whigh, 1)
                act.wait_ge(s_whigh, n + 1)
                nc.scalar.activation(part_stage(n), part_stage(n), ACT.Copy, scale=WSCALE).then_inc(s_w16, 1)

            def other_head_rows(r):
                if r == 0:
                    act.wait_ge(s_pad, 1)
                rows = slice(64 * (1 - r), 64 * (2 - r))
                nc.scalar.activation(KS[rows, :, r, :], pad[rows, 0:1].rearrange("p (a n) -> p a n", a=1).broadcast_to(
                    [64, H // 2, S]), ACT.Copy).then_inc(s_zpad, 1)

            other_head_rows(0)
            for n, t, loaded in ((0, 1, s_wk), (1, 0, s_wq)):
                act.wait_ge(loaded, 16)
                nc.scalar.activation(wh[:, t, :, :], stage[:, t, :, :], ACT.Copy, scale=WSCALE).then_inc(s_wh, 1)
                if n == 0:
                    high_context(0)
            for n, (lo, hi) in enumerate(((0, TT), (TT, TILES))):
                act.wait_ge(s_stats, hi // TT)
                nc.scalar.activation(sd[:, lo:hi], nw[:, 0, lo:hi], ACT.Sqrt).then_inc(s_sqrt, 1)
                if n == 0:
                    other_head_rows(1)
                    act.wait_ge(s_w2, 16 * 2)
                    nc.scalar.activation(wh[:, 2:4, :, :], stage[:, 2:4, :, :], ACT.Copy, scale=WSCALE).then_inc(s_wh, 1)
                    act.wait_ge(s_small, 16 * 4)
                    nc.scalar.activation(tg[:, :], gains[:, :], ACT.Tanh).then_inc(s_tanh, 1)
            high_context(1)
            act.wait_ge(s_zero, 16 * 3)
            parts = {high_slot(n): n for n in range(3 * NE)}
            norms = {second_half(b) + 2: b for b in range(B - 1)}
            choices = {second_half(b) + 5: b for b in range(B - 1)}
            contexts = {context_slot(b): b for b in range(2, B)}
            for n in range(2 * B * SLOTS):
                act.wait_ge(s_score, n + 1)
                if n >= 4:
                    act.wait_ge(s_pv, (n - 4) // 2 + 1)
                nc.scalar.activation(E[:, n % 4, :, :], SC[:, n % 2, :, :], ACT.Exp,
                                     scale=SCORE_SCALE).then_inc(s_exp, 1)
                s, half = divmod(n, 2)
                if half == 1 and s % TT == 0 and s:
                    copy_output(act, s // TT - 1)
                if half == 1 and s in contexts:
                    high_context(contexts[s])
                if half == 1 and s in parts:
                    high_part(parts[s])
                if half == 1 and s in norms:
                    second_norm(norms[s])
                if half == 1 and s in choices:
                    choice_exp(choices[s])
            copy_output(act, B * NG - 1)

            def hidden(i, par):
                act.wait_ge(s_h, i + 1)
                if since(i, 2):
                    act.wait_ge(s_mid, i - 1)
                nc.scalar.activation(silu[:, par, :], HB[:, par, 0, :], ACT.Silu, scale=1.0 / WSCALE).then_inc(s_silu, 1)

            def output(i, par):
                act.wait_ge(s_y, i + 1)
                if since(i, 2):
                    act.wait_ge(s_add, i * 16 - 16)
                nc.scalar.activation(ysb[:, par, :], output_bank(i, par)[:, 0:D], ACT.Copy,
                                     scale=filled[:, bass.ds(i, 1), 1].bitcast(F32)).then_inc(s_ysb, 1)

            def expert_step(i, par):
                if not (isinstance(i, int) and i >= NT):
                    hidden(i, par)
                if since(i, 2):
                    output(i - 2, par)

            for i in range(FIRST):
                expert_step(i, i % 2)
                if i == 1:
                    second_norm(B - 1)
                if i == 4:
                    choice_exp(B - 1)
            with act.Fori(FIRST, NT - 1, 2) as i:
                for o in range(2):
                    expert_step(i + o, o)
            for i in range(NT - 1, NT + 2):
                expert_step(i, i % 2)

        @block.vector
        def _(dve):
            steps = [0]

            def step(ins):
                steps[0] += 1
                ins.then_inc(s_dve, 1)
                dve.wait_ge(s_dve, steps[0])

            def stats(lo, hi, ready):
                for t in range(lo, hi):
                    last = nc.vector.bn_stats(st6[:, t, :], X[:, t, :])
                step(last)
                for t in range(lo, hi):
                    last = nc.vector.bn_aggr(mv[:, t, :], st6[:, t, :])
                step(last)
                nc.vector.tensor_scalar(nw[:, 0, lo:hi], mv[:, lo:hi, 1], EPS, None, ALU.add).then_inc(ready, 1)

            def inverse_deviation(lo, hi, s_root, n):
                dve.wait_ge(s_root, n)
                v, a, r = nw[:, 0, lo:hi], nw[:, 1, lo:hi], rstd[:, lo:hi]
                step(nc.vector.reciprocal(r, sd[:, lo:hi]))
                step(nc.vector.tensor_tensor(a, r, r, ALU.mult))
                step(nc.vector.tensor_tensor(a, a, v, ALU.mult))
                step(nc.vector.tensor_scalar(a, a, -0.5, 1.5, ALU.mult, ALU.add))
                step(nc.vector.tensor_tensor(r, r, a, ALU.mult))

            def normalise(b, ready):
                if ready is s_xn2:
                    dve.wait_ge(s_fill, number["xt", min(b + 2, B - 1), 1] + 1)
                    stored = b
                else:
                    if b:
                        dve.wait_ge(s_fill, number["xt", b - 1, 1] + 1)
                    stored = b - 2
                if stored > 0:
                    dve.wait_ge(s_fill, number["xt2", stored - 1, 1] + 1)
                    dve.wait_ge(s_rows, 16 * stored)
                for t in range(TT):
                    n = TT * b + t
                    last = nc.vector.tensor_scalar(xn[:, t, :], X[:, n, :], mv[:, n, 0:1], rstd[:, n:n + 1],
                                                   ALU.subtract, ALU.mult)
                last.then_inc(ready, 1)

            def split(high, low, src):
                step(nc.vector.tensor_copy(high, src))
                return nc.vector.tensor_tensor(low, src, high, ALU.subtract)

            def low_weights(which, n):
                dve.wait_ge(s_wh, n)
                nc.vector.scalar_tensor_tensor(out=wl[:, which, :, :].rearrange("p a k n -> p (a k n)"),
                                               in0=stage[:, which, :, :].rearrange("p a k n -> p (a k n)"), scalar=WSCALE,
                                               in1=wh[:, which, :, :].rearrange("p a k n -> p (a k n)"),
                                               op0=ALU.mult, op1=ALU.subtract).then_inc(s_wl, 1)

            def choose(b, src, n):
                if b:
                    dve.wait_ge(s_share, b)
                    dve.wait_ge(s_slot, b)
                first = nc.vector.tensor_scalar(lg[:, :, :].rearrange("p t e -> p (t e)"), src[:, 0:TT * NE],
                                                1.0 / WSCALE, None, ALU.mult)
                step(first)
                for t in range(TT):
                    last = nc.vector.max(m8[:, t, :], lg[:, t, :])
                step(last)
                nc.vector.tensor_tensor(gap[:, :], m8[:, :, 1], m8[:, :, 0], ALU.subtract).then_inc(s_gap, 1)
                for t in range(TT):
                    last = nc.vector.max_index(i8[:, t, :], m8[:, t, :], lg[:, t, :])
                step(last)
                step(nc.vector.tensor_copy(idf[:, :, :], i8[:, :, 0:2]))
                for k in range(2):
                    last = nc.vector.tensor_tensor(
                        pick[:, k, TT * b:TT * (b + 1), :], iota_e[:, :].rearrange("p (a e) -> p a e", a=1).broadcast_to([P, TT, NE]),
                        idf[:, :, k:k + 1].broadcast_to([P, TT, NE]), ALU.is_equal)
                step(last)
                return nc.vector.tensor_tensor(both[:, :, :], pick[:, 0, TT * b:TT * (b + 1), :],
                                               pick[:, 1, TT * b:TT * (b + 1), :], ALU.add)

            def weigh_choices(b):
                dve.wait_ge(s_egap, b + 1)
                step(nc.vector.tensor_scalar(den[:, :], egap[:, :], 1.0, None, ALU.add))
                step(nc.vector.reciprocal(den[:, :], den[:, :]))
                step(nc.vector.tensor_scalar(weight[:, TT * b:TT * (b + 1), 0], den[:, :], tg[:, 1:2],
                                             1.0 / (WSCALE * WSCALE), ALU.mult, ALU.mult))
                nc.vector.tensor_tensor(weight[:, TT * b:TT * (b + 1), 1], weight[:, TT * b:TT * (b + 1), 0],
                                        egap[:, :], ALU.mult).then_inc(s_share, 1)

            def number_slots(b, src):
                ranks = src[:, 0:TT * NE].rearrange("p (t e) -> p t e", t=TT)
                step(nc.vector.tensor_tensor(slot_of[:, :, :], ranks, next_slot[:, :].rearrange(
                    "p (a e) -> p a e", a=1).broadcast_to([P, TT, NE]), ALU.add))
                for k in range(2):
                    step(nc.vector.tensor_tensor(chosen[:, :, :], slot_of[:, :, :],
                                                 pick[:, k, TT * b:TT * (b + 1), :], ALU.mult))
                    step(nc.vector.reduce_sum(slots_f[:, k, TT * b:TT * (b + 1)], chosen[:, :, :], AX_X))
                nc.vector.tensor_copy(slot[:, :, TT * b:TT * (b + 1)], slots_f[:, :, TT * b:TT * (b + 1)]).then_inc(s_slot, 1)
                dve.wait_ge(s_slot, b + 1)
                return nc.vector.tensor_tensor(next_slot[:, :], src[:, TT * NE:TT * NE + NE], next_slot[:, :], ALU.add)

            def sums(counts):
                step(nc.vector.tensor_copy(cum[:, 0, :], counts))
                side, reach = 0, 1
                while reach < NE:
                    a, z = cum[:, side, :], cum[:, 1 - side, :]
                    nc.vector.tensor_copy(z[:, 0:reach], a[:, 0:reach])
                    step(nc.vector.tensor_tensor(z[:, reach:NE], a[:, reach:NE], a[:, 0:NE - reach], ALU.add))
                    side, reach = 1 - side, 2 * reach
                return cum[:, side, :]

            def list_tiles(lo, hi):
                first = lo == 0
                n = hi - lo
                emptied(dve, "rank", B - 2 if first else B - 1)
                one = slice(LIST, LIST + 1)
                step(nc.vector.scalar_tensor_tensor(out=cnt[:, :], in0=iota_e[:, :], scalar=-float(REGION),
                                                    in1=next_slot[:, :], op0=ALU.mult, op1=ALU.add))
                step(nc.vector.tensor_scalar(cnt_i[:, 0, :], cnt[:, :], 0.0 if first else float(P - 1), None, ALU.add))
                step(nc.vector.tensor_scalar(cnt_i[:, 1, :], cnt_i[:, 0, :], P.bit_length() - 1, None,
                                             ALU.logical_shift_right))
                step(nc.vector.tensor_copy(ntile[:, :], cnt_i[:, 1, :]))
                if not first:
                    step(nc.vector.tensor_tensor(left[:, :], ntile[:, :], used[:, :], ALU.subtract))
                up_to = sums(ntile[:, :] if first else left[:, :])
                wide = [1, n, NE - 1]
                past, times = before[:, 0, 0:n, :], before[:, 1, 0:n, :]
                step(nc.vector.tensor_tensor(
                    past, up_to[one, 0:NE - 1].rearrange("p (a e) -> p a e", a=1).broadcast_to(wide),
                    iota_t[:, 0:n].rearrange("p (t a) -> p t a", a=1).broadcast_to(wide), ALU.is_le))
                if not first:
                    step(nc.vector.tensor_tensor(ntile[:, 0:NE - 1], ntile[:, 0:NE - 1], used[:, 1:NE], ALU.subtract))
                step(nc.vector.tensor_tensor(times, past, ntile[one, 0:NE - 1].rearrange(
                    "p (a e) -> p a e", a=1).broadcast_to(wide), ALU.mult))
                step(nc.vector.reduce_sum(tile_f[:, 0, 0:n], past, AX_X))
                step(nc.vector.reduce_sum(tile_f[:, 1, 0:n], times, AX_X))
                nc.vector.tensor_copy(tile_e[:, lo:hi], tile_f[:, 0, 0:n])
                step(nc.vector.tensor_tensor(tile_f[:, 2, 0:n], iota_t[:, 0:n], tile_f[:, 1, 0:n], ALU.subtract))
                if not first:
                    step(nc.vector.tensor_scalar(tile_f[:, 2, 0:n], tile_f[:, 2, 0:n], used[one, 0:1], None, ALU.add))
                step(nc.vector.tensor_scalar(tile_f[:, 2, 0:n], tile_f[:, 2, 0:n], float(P), None, ALU.mult))
                nc.vector.scalar_tensor_tensor(out=tile_s[:, lo:hi], in0=tile_f[:, 0, 0:n], scalar=float(REGION),
                                               in1=tile_f[:, 2, 0:n], op0=ALU.mult, op1=ALU.add).then_inc(s_tiles, 1)
                if first:
                    step(nc.vector.tensor_tensor(used[:, :], ntile[:, :], up_to, ALU.subtract))
                    step(nc.vector.tensor_scalar(used[:, :], used[:, :], float(FIRST), 0.0, ALU.add, ALU.max))
                    step(nc.vector.tensor_tensor(used[:, :], used[:, :], ntile[:, :], ALU.min))

            nc.vector.memset(PV[:, :], 0.0).then_inc(s_pz, 1)
            dve.wait_ge(s_x0, 16)
            stats(0, TT, s_stats)
            dve.wait_ge(s_qkbias, 16 * 2)
            step(nc.vector.tensor_scalar(bq_s[:, :, :], bq_s[:, :, :], WSCALE, None, ALU.mult))
            low_weights(slice(1, 2), 1)
            def pad_queries(r):
                nc.vector.memset(QS[64 * r + 32:64 * r + 64, :, :], 0.0).then_inc(s_qpad, 1)

            pad_queries(0)
            inverse_deviation(0, TT, s_sqrt, 1)
            normalise(0, s_xn)
            low_weights(slice(0, 1), 2)

            def empty_entries():
                dve.wait_ge(s_slotno, 1)
                nc.vector.tensor_scalar(empty[:, :, 0], slot_no, P - 1, TOKENS, ALU.bitwise_and,
                                        ALU.bitwise_or).then_inc(s_empty, 1)

            def other_preparations():
                dve.wait_ge(s_tanh, 1)
                step(nc.vector.tensor_scalar(tg16[:, :], tg[:, :], 1.0 / WSCALE, None, ALU.mult))
                nc.vector.tensor_scalar(bo_b[:, :], bo_b[:, :], tg[:, 0:1], None, ALU.mult).then_inc(s_bias, 1)
                dve.wait_ge(s_gate, 16)
                step(nc.vector.tensor_scalar(gh[:, :, :], g32[:, :, :], WSCALE, None, ALU.mult))
                nc.vector.scalar_tensor_tensor(out=gl[:, :, :].rearrange("p k n -> p (k n)"),
                                               in0=g32[:, :, :].rearrange("p k n -> p (k n)"), scalar=WSCALE,
                                               in1=gh[:, :, :].rearrange("p k n -> p (k n)"),
                                               op0=ALU.mult, op1=ALU.subtract).then_inc(s_gsplit, 1)
                dve.wait_ge(s_const, 1)

            def second_normalise(b):
                inverse_deviation(TT * b, TT * (b + 1), s_sqrt2, b + 1)
                normalise(b, s_xn2)

            def finish(n):
                u = order[n]
                kind, b = u[0], u[1]
                if n and order[n - 1] == ("mt", 0, 0):
                    other_preparations()
                    inverse_deviation(TT, TILES, s_sqrt, 2)
                if kind == "xt" and u[2] == 0 and b:
                    normalise(b, s_xn)
                if u == ("k", 0, 1):
                    pad_queries(1)
                if u == ("q", 0, 1):
                    empty_entries()
                if u == ("q", 0, 0):
                    low_weights(slice(2, 4), 3)
                if u == ("v", 0, 0):
                    dve.wait_ge(s_x, 16)
                early_stats = [("v", 0, 0), ("v", 0, 1), ("max", 0, 0, 0, 0)]
                if u in early_stats:
                    t = TT * (early_stats.index(u) + 1)
                    stats(t, t + TT, s_stats)
                if kind == "xt2" and u[2] == 0 and b < B - 1:
                    second_normalise(b)
                dve.wait_ge(s_fill, n + 1)
                src = WB[:, (n % NB if n < LATE else 0), :]
                if kind in ("xt", "at", "xt2") and n:
                    dve.wait_ge(s_free, n)
                if kind == "xt":
                    last = split(xth[:, u[2], :], xtl[:, u[2], :], src)
                elif kind in "qk":
                    t, c = "qk".index(kind), u[2]
                    if b and t == 1 and c == 0:
                        for g in range(NG):
                            dve.wait_ge(s_stack[g], 16 * 12 * b)
                    high, low = nat[:, t, 0, c, :], nat[:, t, 1, c, :]
                    step(nc.vector.tensor_scalar(high, src, bq_s[:, t, c:c + 1], None, ALU.add))
                    last = nc.vector.scalar_tensor_tensor(out=low, in0=src, scalar=bq_s[:, t, c:c + 1], in1=high,
                                                          op0=ALU.add, op1=ALU.subtract)
                elif kind == "v":
                    if b == 0:
                        dve.wait_ge(s_vone, 1)
                        dve.wait_ge(s_small, 16 * 4)
                    if b >= 2 and u[2] == 0:
                        dve.wait_ge(s_pv, SLOTS * (b - 1))
                    for tt in range(2):
                        last = nc.vector.scalar_tensor_tensor(
                            out=V[:, b % 2, 2 * u[2] + tt, :, 0:DH],
                            in0=src[:, D * tt:D * (tt + 1)].rearrange("p (h d) -> p h d", h=H), scalar=1.0 / WSCALE,
                            in1=bv_b[:, :].rearrange("p (h d) -> p h d", h=H), op0=ALU.mult, op1=ALU.add)
                elif kind == "max":
                    _, _, g, tt, j = u
                    last = nc.vector.reduce_max(mx[:, g % 2, tt, (j % 2) * 2 + j // 2:(j % 2) * 2 + j // 2 + 1],
                                                src, AX_X)
                elif kind == "mt":
                    g = u[2]
                    if b:
                        dve.wait_ge(s_mrow[g], 32 * b)
                    if b:
                        last = nc.vector.scalar_tensor_tensor(out=mrow[:, g, :], in0=src[0:G, :],
                                                              scalar=1.0 / MSCALE, in1=mrow[:, g, :],
                                                              op0=ALU.mult, op1=ALU.add)
                    else:
                        last = nc.vector.tensor_scalar(mrow[:, g, :], src[0:G, :], 1.0 / MSCALE, None, ALU.mult)
                elif kind == "ot":
                    g = u[2]
                    o = src.rearrange("p (t j w) -> p t j w", t=TT, j=G)
                    if b and g == 0:
                        dve.wait_ge(s_fill, number["at", b - 1, 1] + 1)
                    if b or g:
                        emptied(dve, "ot", b - (g == 0), (g - 1) % NG)
                    step(nc.vector.reciprocal(rec[:, :, :], o[:, :, :, DH]))
                    last = nc.vector.tensor_tensor(
                        att[:, :, G * DH * g:G * DH * (g + 1)].rearrange("p t (j d) -> p t j d", j=G),
                        o[:, :, :, 0:DH],
                        rec[:, :, :].rearrange("p t (j a) -> p t j a", a=1).broadcast_to([P, TT, G, DH]), ALU.mult)
                elif kind == "at":
                    last = split(ath[:, u[2], :], atl[:, u[2], :], src)
                elif kind == "wo":
                    if u[2] == 0:
                        dve.wait_ge(s_xbo, b + 1)
                    rows = X[:, TT * b + 2 * u[2]:TT * b + 2 * u[2] + 2, :].rearrange("p t d -> p (t d)")
                    last = nc.vector.scalar_tensor_tensor(out=rows, in0=src, scalar=tg16[:, 0:1], in1=rows,
                                                          op0=ALU.mult, op1=ALU.add)
                elif kind == "xt2":
                    last = split(ath[:, u[2], :], atl[:, u[2], :], src)
                elif kind == "gate":
                    last = choose(b, src, n)
                elif kind == "rank":
                    weigh_choices(b)
                    last = number_slots(b, src)
                last.then_inc(s_free, 1)
                if kind == "wo" and u[2] == 1:
                    dve.wait_ge(s_free, n + 1)
                    stats(TT * b, TT * (b + 1), s_stats2)
                if u == ("rank", B - 2):
                    list_tiles(0, FIRST)

            for n in range(LATE):
                finish(n)

            def tile_split(i, par):
                dve.wait_ge(s_tx, i + 1)
                if since(i, 2):
                    dve.wait_ge(s_h, i - 1)
                nc.vector.tensor_copy(xs[:, par, 0, :], TX[:, 0:D]).then_inc(s_xhigh, 1)
                dve.wait_ge(s_xhigh, i + 1)
                nc.vector.tensor_tensor(xs[:, par, 1, :], TX[:, 0:D], xs[:, par, 0, :], ALU.subtract).then_inc(s_xs, 1)

            def middle(i, par):
                dve.wait_ge(s_silu, i + 1)
                if since(i, 2):
                    dve.wait_ge(s_tm, i - 1)
                nc.vector.tensor_tensor(mid[:, par, :], HB[:, par, 1, :], silu[:, par, :], ALU.mult).then_inc(s_mid, 1)

            def middle_split(i, par):
                dve.wait_ge(s_tm, i + 1)
                if since(i, 2):
                    dve.wait_ge(s_y, i - 1)
                nc.vector.tensor_copy(ms[:, par, 0, :], TM).then_inc(s_mhigh, 1)
                dve.wait_ge(s_mhigh, i + 1)
                nc.vector.tensor_tensor(ms[:, par, 1, :], TM, ms[:, par, 0, :], ALU.subtract).then_inc(s_ms, 1)

            def expert_step(i, par):
                if not (isinstance(i, int) and i >= NT - 1):
                    tile_split(i + 1, 1 - par)
                if since(i, 1):
                    middle_split(i - 1, 1 - par)
                if not (isinstance(i, int) and i >= NT):
                    middle(i, par)

            for u in after_tile[-1]:
                finish(number[u])
            tile_split(0, 0)
            for i in range(FIRST):
                expert_step(i, i % 2)
                if i == 1:
                    second_normalise(B - 1)
                for u in after_tile.get(i, []):
                    finish(number[u])
                if i == LISTED:
                    list_tiles(FIRST, NT)
            with dve.Fori(FIRST, NT - 1, 2) as i:
                for o in range(2):
                    expert_step(i + o, o)
            for i in range(NT - 1, NT + 1):
                expert_step(i, i % 2)
        @block.tensor
        def _(pe):
            count = [0]

            def three(dst, sh, sl, mh, ml, first, last):
                nc.tensor.matmul(dst, sh, mh, start=first, stop=False)
                nc.tensor.matmul(dst, sh, ml, start=False, stop=False)
                return nc.tensor.matmul(dst, sl, mh, start=False, stop=last)

            def unit(u):
                n = count[0]
                count[0] += 1
                assert order[n] == u
                kind, b = u[0], u[1]
                if n >= LATE:
                    pe.wait_ge(s_free, n)
                elif n >= NB:
                    pe.wait_ge(s_free, n - NB + 1)
                dst = WB[:, (n % NB if n < LATE else 0), :]
                if kind == "xt":
                    pe.wait_ge(s_xn, b + 1)
                    for t in range(TT):
                        last = nc.tensor.transpose(dst[:, P * t:P * (t + 1)], xn[:, t, P * u[2]:P * (u[2] + 1)], ident[:, :])
                elif kind in "qk":
                    t, c = "qk".index(kind), u[2]
                    if kind == "q":
                        emptied(pe, "xt", b, 1)
                    else:
                        pe.wait_ge(s_ctsplit, b + 1)
                    if b == 0:
                        pe.wait_ge(s_wl, 2 - t)
                    mh, ml = ((xth, xtl), (cth, ctl))[t]
                    for k in range(KD):
                        last = three(dst, wh[:, t, k, P * c:P * (c + 1)], wl[:, t, k, P * c:P * (c + 1)],
                                     mh[:, k, :], ml[:, k, :], k == 0, k == KD - 1)
                elif kind == "v":
                    if b == 0:
                        pe.wait_ge(s_wl, 3)
                    for tt in range(2):
                        tok = slice(P * (2 * u[2] + tt), P * (2 * u[2] + tt + 1))
                        for k in range(KD):
                            last = three(dst[:, D * tt:D * (tt + 1)], cth[:, k, tok], ctl[:, k, tok],
                                         wh[:, 2, k, :], wl[:, 2, k, :], k == 0, k == KD - 1)
                elif kind == "max":
                    _, _, g, tt, j = u
                    if (tt, j) == (0, 0):
                        pe.wait_ge(s_stack[g], 16 * 12 * (b + 1))
                    r, pair = j % 2, 2 * g + j // 2
                    last = nc.tensor.matmul(dst, QS[:, pair, P * tt:P * (tt + 1)],
                                            KS[:, pair, r, :], start=True, stop=True)
                elif kind == "mt":
                    g = u[2]
                    emptied(pe, "max", b, g, TT - 1, G - 1)
                    for t in range(TT):
                        last = nc.tensor.transpose(dst[0:G, P * t:P * (t + 1)], mx[:, g % 2, t, :], ident[:, :])
                elif kind == "ot":
                    q = NG * b + u[2]
                    pe.wait_ge(s_ot, q + 1)
                    for t in range(TT):
                        last = nc.tensor.transpose(dst[:, P * t:P * (t + 1)], OT[:, q % 2, P * t:P * (t + 1)], ident[:, :])
                elif kind == "at":
                    emptied(pe, "ot", b, NG - 1)
                    for t in range(TT):
                        last = nc.tensor.transpose(dst[:, P * t:P * (t + 1)], att[:, t, P * u[2]:P * (u[2] + 1)], ident[:, :])
                elif kind == "wo":
                    emptied(pe, "at", b, 1)
                    for tt in range(2):
                        tok = slice(P * (2 * u[2] + tt), P * (2 * u[2] + tt + 1))
                        for k in range(KD):
                            last = three(dst[:, D * tt:D * (tt + 1)], ath[:, k, tok], atl[:, k, tok],
                                         wh[:, 3, k, :], wl[:, 3, k, :], k == 0, k == KD - 1)
                elif kind == "xt2":
                    pe.wait_ge(s_xn2, b + 1)
                    for t in range(TT):
                        last = nc.tensor.transpose(dst[:, P * t:P * (t + 1)], xn[:, t, P * u[2]:P * (u[2] + 1)], ident[:, :])
                elif kind == "gate":
                    emptied(pe, "xt2", b, 1)
                    if b == 0:
                        pe.wait_ge(s_gsplit, 1)
                    for t in range(TT):
                        for k in range(KD):
                            last = three(dst[:, NE * t:NE * (t + 1)], ath[:, k, P * t:P * (t + 1)],
                                         atl[:, k, P * t:P * (t + 1)], gh[:, k, :], gl[:, k, :], k == 0, k == KD - 1)
                elif kind == "rank":
                    emptied(pe, "gate", b)
                    if b == 0:
                        pe.wait_ge(s_const, 1)
                    for t in range(TT + 1):
                        for a in range(min(t + 1, TT)):
                            last = nc.tensor.matmul(dst[:, NE * t:NE * (t + 1)], (earlier if a == t else ones)[:, :],
                                                    both[:, a, :], start=(a == 0), stop=(a == min(t, TT - 1)))
                last.then_inc(s_fill, 1)

            def scores(n):
                s, pp = divmod(n, 2)
                b, s = divmod(s, SLOTS)
                g, st = divmod(s, TT)
                if (st, pp) == (0, 0):
                    pe.wait_ge(s_mrow[g], 32 * (b + 1))
                if n >= 2:
                    pe.wait_ge(s_exp, n - 1)
                for r in range(2):
                    last = nc.tensor.matmul(SC[:, n % 2, r, :], KS[:, 2 * g + pp, r, P * st:P * (st + 1)],
                                            QS[:, 2 * g + pp, :], start=True, stop=True)
                last.then_inc(s_score, 1)

            def weigh(s):
                b, q = divmod(s, SLOTS)
                g, st = divmod(q, TT)
                pe.wait_ge(s_exp, 2 * s + 2)
                if st == 0 and s:
                    pe.wait_ge(s_ot, s // TT)
                if st == 0 and g == 0:
                    emptied(pe, "v", b, 1)
                for j in range(G):
                    last = nc.tensor.matmul(PV[32 * j:32 * j + VW, :], V[:, b % 2, st, G * g + j, :],
                                            E[:, (2 * s + j // 2) % 4, j % 2, :], start=(st == 0), stop=(st == TT - 1))
                last.then_inc(s_pv, 1)

            pe.wait_ge(s_ident, 1)
            pe.wait_ge(s_pz, 1)
            for u in slot_units[-1]:
                unit(u)
            scores(0)
            scores(1)
            for s in range(B * SLOTS):
                units = slot_units[s]
                one, two = len(units) * 5 // 12, len(units) * 8 // 12
                for u in units[:one]:
                    unit(u)
                if s + 1 < B * SLOTS:
                    scores(2 * s + 2)
                for u in units[one:two]:
                    unit(u)
                if s + 1 < B * SLOTS:
                    scores(2 * s + 3)
                for u in units[two:]:
                    unit(u)
                weigh(s)
            for u in after_tile[-1]:
                unit(u)

            def turn_tile(i, par):
                pe.wait_ge(s_xg[par], i * 8 - 8 * par + 16)
                if since(i, 1):
                    pe.wait_ge(s_xs, i)
                for k in range(KD):
                    last = nc.tensor.transpose(TX[:, P * k:P * (k + 1)], xg[:, par, P * k:P * (k + 1)], ident[:, :])
                last.then_inc(s_tx, 1)

            def hidden(i, par, e):
                pe.wait_ge(s_xs, i + 1)
                if since(i, 2):
                    pe.wait_ge(s_mid, i - 1)
                for k in range(KD):
                    xh, xl = (xs[:, par, h, P * k:P * (k + 1)] for h in range(2))
                    for m in range(2):
                        high, low = (WE[:, bass.ds(e, 1), 2 * m + h, HID * k:HID * (k + 1)].rearrange(
                            "p a n -> p (a n)") for h in range(2))
                        last = three(HB[:, par, m, :], xh, xl, high, low, k == 0, k == KD - 1)
                last.then_inc(s_h, 1)

            def turn_middle(i, par):
                pe.wait_ge(s_mid, i + 1)
                if since(i, 1):
                    pe.wait_ge(s_ms, i)
                for k in range(KH):
                    last = nc.tensor.transpose(TM[:, P * k:P * (k + 1)], mid[:, par, P * k:P * (k + 1)], ident[:, :])
                last.then_inc(s_tm, 1)

            def output(i, par, e):
                pe.wait_ge(s_ms, i + 1)
                if isinstance(i, int) and 0 < i < FIRST - 2:
                    pe.wait_ge(s_ysb, i)
                elif since(i, 2):
                    pe.wait_ge(s_ysb, i - 1)
                for k in range(KH):
                    mh, ml = (ms[:, par, h, P * k:P * (k + 1)] for h in range(2))
                    high, low = (WE[:, bass.ds(e, 1), 4 + h, D * k:D * (k + 1)].rearrange(
                        "p a n -> p (a n)") for h in range(2))
                    last = three(output_bank(i, par)[:, 0:D], mh, ml, high, low, k == 0, k == KH - 1)
                last.then_inc(s_y, 1)

            def expert(i):
                return pe.value_load(tile_e[0:1, bass.ds(i, 1)], min_val=0, max_val=NE - 1)

            pe.wait_ge(s_tiles, 1)
            pe.wait_ge(s_wsplit, 3 * NE)
            def expert_step(i, par):
                if not (isinstance(i, int) and i >= NT):
                    hidden(i, par, expert(i))
                if not (isinstance(i, int) and i >= NT - 1):
                    turn_tile(i + 1, 1 - par)
                if since(i, 1) and not (isinstance(i, int) and i > NT):
                    turn_middle(i - 1, 1 - par)
                if since(i, 2):
                    output(i - 2, par, expert(i - 2))

            turn_tile(0, 0)
            for i in range(FIRST):
                if i == FIRST - 2:
                    pe.wait_ge(s_tiles, 2)
                expert_step(i, i % 2)
                for u in after_tile.get(i, []):
                    unit(u)
            pe.wait_ge(s_free, len(order))
            with pe.Fori(FIRST, NT - 1, 2) as i:
                for o in range(2):
                    expert_step(i + o, o)
            for i in range(NT - 1, NT + 2):
                expert_step(i, i % 2)


_NAMES = ["x", "ctxT", "g_xattn", "g_ffn", "wq", "bq", "wk", "bk", "wv", "bv", "woT", "bo", "gate", "w0", "w1", "wo"]


def kernel(x, ctx_1024, g_xattn, g_ffn, L0_xattn_Wq, L0_xattn_bq, L0_xattn_Wk, L0_xattn_bk, L0_xattn_Wv, L0_xattn_bv,
           L0_xattn_Wo, L0_xattn_bo, L0_ffn_gate_kernel, L0_ffn_w0_kernel, L0_ffn_w1_kernel, L0_ffn_wo_kernel):
    import numpy as np
    import concourse.bacc as bacc
    from concourse import mybir as mb
    from concourse.bass_utils import run_bass_kernel_spmd

    def packed(a):
        return np.ascontiguousarray(np.asarray(a))

    B, S, D = x.shape
    H, _, DH = L0_xattn_Wq.shape
    heads = [2 * (2 * (i // 2) + c) + i % 2 for c in range(2) for i in range(H // 2)]

    def columns(w, order):
        return packed(np.asarray(w)[order].transpose(1, 0, 2).reshape(D, H * DH))

    arrays = {
        "x": packed(x).reshape(B * S, D),
        "ctxT": packed(np.asarray(ctx_1024).transpose(0, 2, 1)),
        "g_xattn": packed(g_xattn), "g_ffn": packed(g_ffn),
        "wq": columns(L0_xattn_Wq, heads), "bq": packed(np.asarray(L0_xattn_bq)[heads].reshape(2, -1).T),
        "wk": columns(L0_xattn_Wk, heads), "bk": packed(np.asarray(L0_xattn_bk)[heads].reshape(2, -1).T),
        "wv": columns(L0_xattn_Wv, list(range(H))), "bv": packed(np.asarray(L0_xattn_bv).reshape(-1)),
        "woT": packed(np.asarray(L0_xattn_Wo).T), "bo": packed(L0_xattn_bo),
        "gate": packed(L0_ffn_gate_kernel),
        "w0": packed(L0_ffn_w0_kernel), "w1": packed(L0_ffn_w1_kernel), "wo": packed(L0_ffn_wo_kernel),
    }
    arrays["g_xattn"] = arrays["g_xattn"].reshape(-1)
    arrays["g_ffn"] = arrays["g_ffn"].reshape(-1)
    nc = bacc.Bacc("TRN2", target_bir_lowering=False, num_devices=1)
    aps = [nc.dram_tensor(f"in_{n}", arrays[n].shape, mb.dt.from_np(arrays[n].dtype), kind="ExternalInput").ap()
           for n in _NAMES]
    out = nc.dram_tensor("out", (B * S + P, D), mb.dt.float32, kind="ExternalOutput").ap()
    program(nc, *aps, out)
    r = run_bass_kernel_spmd(nc, [{f"in_{n}": arrays[n] for n in _NAMES}], core_ids=[0])
    return r.results[0]["out"][:B * S].reshape(B, S, D)
```
